# Optimizing a Trainium2 kernel written in Bass

```python
import numpy as np
import jax
import jax.numpy as jnp

def _softmax(x, axis=-1):
    return jax.nn.softmax(x, axis=axis)

def _gelu(x):
    return jax.nn.gelu(x, approximate=True)

def _silu(x):
    return jax.nn.silu(x)

def _sigmoid(x):
    return jax.nn.sigmoid(x)

def _layernorm(x, axis=-1, eps=1e-05):
    m = jnp.mean(x, axis=axis, keepdims=True)
    v = jnp.var(x, axis=axis, keepdims=True)
    return (x - m) / jnp.sqrt(v + eps)

def _scatter_add(tgt, idx, src, axis=0):
    return tgt.at[idx].add(src)

def _segment_sum(src, seg, n):
    return jax.ops.segment_sum(src, seg, n)
kernel_name = 'mk_macaron_d1_jaxref_r8_a003cd'

def setup_inputs(seed: int=0):
    np.random.seed(seed)
    _w = jnp.asarray

    def _L0_attn_setup():
        import jax, jax.numpy as jnp
        import numpy as np
        B, T = (4, 256)
        D_MODEL = 128
        N_HEADS = 8
        HEAD_DIM = 32
        KV_LRANK = 64

        def _orthogonalize_per_head(w):
            chunks = w.reshape(N_HEADS, HEAD_DIM, D_MODEL)

            def ns(m):
                A = m @ m.T
                Bm = 1.5 * jnp.eye(HEAD_DIM, dtype=m.dtype) - 0.5 * A
                return Bm @ m
            return jax.vmap(ns)(chunks).reshape(w.shape)
        key = jax.random.key(seed)
        ks = jax.random.split(key, 6)

        def lin(k, out_dim, in_dim):
            bound = 1.0 / np.sqrt(in_dim)
            return jax.random.uniform(k, (out_dim, in_dim), jnp.float32, -bound, bound)
        Wq = _orthogonalize_per_head(lin(ks[0], N_HEADS * HEAD_DIM, D_MODEL))
        return {'x': jax.random.normal(ks[1], (B, T, D_MODEL), jnp.float32), 'Wq': Wq, 'Wkv_down': lin(ks[2], KV_LRANK, D_MODEL), 'Wk_up': lin(ks[3], N_HEADS * HEAD_DIM, KV_LRANK), 'Wv_up': lin(ks[4], N_HEADS * HEAD_DIM, KV_LRANK), 'Wo': lin(ks[5], D_MODEL, N_HEADS * HEAD_DIM)}
    _L0_attn_in = _L0_attn_setup()

    def _L0_ffn_setup():
        import jax, jax.numpy as jnp
        import numpy as np
        B, S, D, H, O, E, K = (4, 256, 128, 256, 128, 8, 2)
        key = jax.random.key(seed)
        ks = jax.random.split(key, 8)
        x = jax.random.normal(ks[0], (B, S, D), dtype=jnp.float32)
        gate_w = jax.random.uniform(ks[1], (E, D), dtype=jnp.float32, minval=-1, maxval=1) * np.sqrt(6.0 / D)
        gate_b = jnp.zeros((E,), dtype=jnp.float32)
        w1 = jax.random.uniform(ks[2], (E, D, H), dtype=jnp.float32, minval=-1, maxval=1) * np.sqrt(6.0 / D)
        b1 = jnp.zeros((E, H), dtype=jnp.float32)
        w2 = jax.random.uniform(ks[3], (E, H, O), dtype=jnp.float32, minval=-1, maxval=1) * np.sqrt(6.0 / H)
        b2 = jnp.zeros((E, O), dtype=jnp.float32)
        return {'x': x, 'gate_w': gate_w, 'gate_b': gate_b, 'w1': w1, 'b1': b1, 'w2': w2, 'b2': b2}
    _L0_ffn_in = _L0_ffn_setup()
    _d = {'L0_attn_x': _L0_attn_in['x'], 'L0_attn_Wq': _L0_attn_in['Wq'], 'L0_attn_Wkv_down': _L0_attn_in['Wkv_down'], 'L0_attn_Wk_up': _L0_attn_in['Wk_up'], 'L0_attn_Wv_up': _L0_attn_in['Wv_up'], 'L0_attn_Wo': _L0_attn_in['Wo'], 'L0_ffn_gate_w': _L0_ffn_in['gate_w'], 'L0_ffn_gate_b': _L0_ffn_in['gate_b'], 'L0_ffn_w1': _L0_ffn_in['w1'], 'L0_ffn_b1': _L0_ffn_in['b1'], 'L0_ffn_w2': _L0_ffn_in['w2'], 'L0_ffn_b2': _L0_ffn_in['b2']}
    _x0 = _d['L0_attn_x']
    _d['L0_attn_x'] = jax.random.normal(jax.random.fold_in(jax.random.key(seed), 1), (16, 512, 128), dtype=_x0.dtype)
    del _x0
    return _d

def reference(L0_attn_x, L0_attn_Wq, L0_attn_Wkv_down, L0_attn_Wk_up, L0_attn_Wv_up, L0_attn_Wo, L0_ffn_gate_w, L0_ffn_gate_b, L0_ffn_w1, L0_ffn_b1, L0_ffn_w2, L0_ffn_b2):

    def _L0_attn_ref(x, Wq, Wkv_down, Wk_up, Wv_up, Wo):
        import jax, jax.numpy as jnp
        import numpy as np
        B, T = (4, 256)
        D_MODEL = 128
        N_HEADS = 8
        HEAD_DIM = 32
        KV_LRANK = 64

        def _orthogonalize_per_head(w):
            chunks = w.reshape(N_HEADS, HEAD_DIM, D_MODEL)

            def ns(m):
                A = m @ m.T
                Bm = 1.5 * jnp.eye(HEAD_DIM, dtype=m.dtype) - 0.5 * A
                return Bm @ m
            return jax.vmap(ns)(chunks).reshape(w.shape)
        b, t, _ = x.shape
        q = (x @ Wq.T).reshape(b, t, N_HEADS, HEAD_DIM)
        kv_latent = x @ Wkv_down.T
        k = (kv_latent @ Wk_up.T).reshape(b, t, N_HEADS, HEAD_DIM)
        v = (kv_latent @ Wv_up.T).reshape(b, t, N_HEADS, HEAD_DIM)
        scale = HEAD_DIM ** (-0.5)
        scores = jnp.einsum('bqhd,bkhd->bhqk', q, k) * scale
        attn = jax.nn.softmax(scores, axis=-1)
        out = jnp.einsum('bhqk,bkhd->bqhd', attn, v)
        out = out.reshape(b, t, N_HEADS * HEAD_DIM)
        return out @ Wo.T

    def _L0_ffn_ref(x, gate_w, gate_b, w1, b1, w2, b2):
        import jax, jax.numpy as jnp
        import numpy as np
        B, S, D, H, O, E, K = (4, 256, 128, 256, 128, 8, 2)
        logits = jnp.einsum('bsd,ed->bse', x, gate_w) + gate_b
        probs = jax.nn.softmax(logits, axis=-1)
        topk_vals, topk_idx = jax.lax.top_k(probs, K)
        h = jax.nn.relu(jnp.einsum('bsd,edh->bseh', x, w1) + b1)
        expert_out = jnp.einsum('bseh,eho->bseo', h, w2) + b2
        sel = jnp.take_along_axis(expert_out, topk_idx[..., None], axis=2)
        return jnp.sum(sel * topk_vals[..., None], axis=2)
    x = L0_attn_x
    x = x + 0.5 * _L0_ffn_ref(_layernorm(x, axis=-1), L0_ffn_gate_w, L0_ffn_gate_b, L0_ffn_w1, L0_ffn_b1, L0_ffn_w2, L0_ffn_b2)
    x = x + _L0_attn_ref(_layernorm(x, axis=-1), L0_attn_Wq, L0_attn_Wkv_down, L0_attn_Wk_up, L0_attn_Wv_up, L0_attn_Wo)
    x = x + 0.5 * _L0_ffn_ref(_layernorm(x, axis=-1), L0_ffn_gate_w, L0_ffn_gate_b, L0_ffn_w1, L0_ffn_b1, L0_ffn_w2, L0_ffn_b2)
    return x

_drawn_inputs = setup_inputs


def setup_inputs(seed=0):
    import zlib

    import numpy as np

    out = dict(_drawn_inputs(seed))
    spreads = {'L0_ffn_gate_b': (0.0, 0.1), 'L0_ffn_b1': (0.0, 0.1), 'L0_ffn_b2': (0.0, 0.1)}
    factors = {'L0_attn_Wq': 4.04, 'L0_attn_Wk_up': 3.886}
    for name, (base, spread) in spreads.items():
        noise = np.random.default_rng([zlib.crc32(name.encode()), seed]).standard_normal(out[name].shape)
        drawn = base * np.exp(spread * noise) if base else spread * noise
        out[name] = jnp.asarray(drawn.astype(out[name].dtype))
    for name, factor in factors.items():
        out[name] = (out[name] * factor).astype(out[name].dtype)
    return out
```

```python
from contextlib import ExitStack

import concourse.bass as bass
from concourse import mybir
from concourse.alu_op_type import AluOpType as ALU

F32 = mybir.dt.float32
F32R = mybir.dt.float32r
I32 = mybir.dt.int32
ACT = mybir.ActivationFunctionType
AX = mybir.AxisListType

P = 128
EPS = 1e-5
RSQRT_MAGIC = 0x5F3759DF
NEWTON_STEPS = 3

EXPERTS, UNITS = 8, 16
TILES, HEADS, GROUP = 4, 8, 4
GROUPS = HEADS // GROUP


def ffn_steps(s, b):
    steps = [(s, b, "norm", 0), (s, b, "xT", 0), (s, b, "logits", 0), (s, b, "gT", 0), (s, b, "gb", 0)]
    lag = 3
    for u in range(UNITS + lag):
        if u < UNITS:
            if u % 2 == 0 and u // 2 + 1 < EXPERTS:
                steps.append((s, b, "gb", u // 2 + 1))
            steps.append((s, b, "h", u))
        if u >= lag:
            steps.append((s, b, "y", u - lag))
    return steps + [(s, b, "fix", 0), (s, b, "back", 0)]


def attention_steps(b):
    s = "B"
    steps = [(s, b, "norm", 0), (s, b, "xT", 0)] + [(s, b, n, g) for g in range(GROUPS) for n in ("q", "k")]
    steps += [(s, b, "v", n) for n in range(2)]
    steps += [(s, b, "max", n) for n in range(HEADS * TILES)] + [(s, b, "mrow", 0)]
    for g in range(GROUPS):
        for kt in range(TILES):
            steps += [(s, b, "s", (g * TILES + kt) * GROUP + j) for j in range(GROUP)]
            if kt:
                steps += [(s, b, "pv", g * TILES + kt - 1), (s, b, "add", g * TILES + kt)]
        steps += [(s, b, "pv", g * TILES + TILES - 1), (s, b, "sum", g), (s, b, "onorm", g)]
    return steps + [(s, b, "wo", 0), (s, b, "back", 0)]


ADDS = {
    "d_full": {"xT": 1, "logits": 2, "gT": 1, "h": 1, "back": 1, "q": 1, "k": 1, "max": 1, "mrow": 2, "sum": 1},
    "a_full": {"gb": 1, "v": 1, "s": 1, "wo": 1},
    "xn_done": {"norm": 1},
    "lg_done": {"logits": 1},
    "ex_done": {"logits": 1},
    "g_done": {"logits": 1},
    "hh_done": {"h": 1},
    "hl_done": {"h": 1},
    "y_used": {"y": 1},
    "y_full": {"fix": 1},
    "yT_done": {"fix": 1},
    "q_stacked": {"q": 16 * 3 * GROUP},
    "k_stacked": {"k": 16 * 3 * GROUP},
    "m_stacked": {"mrow": 32},
    "p_used": {"pv": 1},
    "p_added": {"add": 1},
    "o_read": {"onorm": 1},
    "o_done": {"onorm": 1},
    "x_in": {"load": 16},
    "x_out": {"store": 16},
}
ADDS["d_done"] = ADDS["d_full"]
ADDS["a_done"] = ADDS["a_full"]


def macaron_kernel(nc, x, wq, wkv_down, wk_up, wv_up, wo, gate_w, gate_b, w1, b1, w2, b2, out):
    BATCHES, TOKENS, D = x.shape
    HID = w1.shape[2]
    RANK = wkv_down.shape[0]
    HD = wq.shape[0]
    DH = HD // HEADS
    SCALE = float(DH) ** -0.5
    assert D == P and TOKENS == TILES * P and HID == 2 * P and HD == GROUPS * P and w1.shape[0] == EXPERTS
    STACK = 3 * DH
    KROWS = STACK + 2
    GROWS = 72
    D_RING, A_RING = 3, 3
    H_RING, GB_RING, P_RING = 4, 4, 2

    def batch_steps(b):
        return ffn_steps("A", b) + [("A", b, "load", 0)] + attention_steps(b) + ffn_steps("C", b) + [("C", b, "store", 0)]

    first, body, last = batch_steps(0), batch_steps(1), batch_steps(BATCHES - 1)
    LOOP0, LOOPS = 1, BATCHES - 2
    per_body = {sem: sum(adds.get(st[2], 0) for st in body) for sem, adds in ADDS.items()}
    assert per_body["d_full"] % D_RING == 0 and per_body["a_full"] % A_RING == 0
    counts = {}
    for sem, adds in ADDS.items():
        n = 0
        for st in first + body:
            n += adds.get(st[2], 0)
            if st[2] in adds:
                counts[sem, st] = n
        n += (LOOPS - 1) * per_body[sem]
        for st in last:
            n += adds.get(st[2], 0)
            if st[2] in adds:
                counts[sem, st] = n

    with ExitStack() as ctx:
        def sb(name, shape, dt=F32):
            return ctx.enter_context(nc.sbuf_tensor(name, shape, dt))

        def sem(name):
            return ctx.enter_context(nc.semaphore(name))

        x_of = {n: sb("x_" + n, [P, TILES, D]) for n in ("in", "A", "B", "C")}
        x_before = {"A": x_of["in"], "B": x_of["A"], "C": x_of["B"]}
        w1h, w1l = sb("w1h", [P, EXPERTS * HID], F32R), sb("w1l", [P, EXPERTS * HID], F32R)
        w2h, w2l = sb("w2h", [P, UNITS, D], F32R), sb("w2l", [P, UNITS, D], F32R)
        wqkv_h, wqkv_l = sb("wqkv_h", [P, 3, HD], F32R), sb("wqkv_l", [P, 3, HD], F32R)
        wo_h, wo_l = sb("wo_h", [P, GROUPS, D], F32R), sb("wo_l", [P, GROUPS, D], F32R)
        gw_h, gw_l = sb("gw_h", [P, EXPERTS], F32R), sb("gw_l", [P, EXPERTS], F32R)
        neg_b1 = sb("neg_b1", [P, UNITS])
        b1_masked = sb("b1_masked", [P, UNITS, EXPERTS])
        gate_bias = sb("gate_bias", [P, TILES, EXPERTS])
        first_wins = sb("first_wins", [P, TILES, EXPERTS])
        b2_sb = sb("b2_sb", [EXPERTS, D])
        corr_f = sb("corr_f", [EXPERTS, D])
        corr = sb("corr", [GROWS, D], F32R)
        pick_f = sb("pick_f", [GROWS, EXPERTS, P])
        pick = sb("pick", [GROWS, EXPERTS, P], F32R)
        ident = sb("ident", [P, P])
        ones = sb("ones", [P, DH])
        up_T = sb("up_T", [RANK, 2 * HD])
        stats, mv = sb("stats", [P, TILES, 6]), sb("mv", [P, TILES, 2])
        veps, rstd, nt = sb("veps", [P, TILES]), sb("rstd", [P, TILES]), sb("nt", [P, TILES])
        half_bits = sb("half_bits", [P, TILES], I32)
        xn = sb("xn", [P, TILES, D])
        xT_h, xT_l = sb("xT_h", [P, TOKENS], F32R), sb("xT_l", [P, TOKENS], F32R)
        lg, ex, pr = (sb(n, [P, TILES, EXPERTS]) for n in ("lg", "ex", "pr"))
        eq, cand, one1, one2, pr2, G = (sb(n, [P, TILES, EXPERTS]) for n in ("eq", "cand", "one1", "one2", "pr2", "G"))
        mx, sm, rs, m1, s1, m2, s2 = (sb(n, [P, TILES]) for n in ("mx", "sm", "rs", "m1", "s1", "m2", "s2"))
        gT = sb("gT", [GROWS, TOKENS], F32R)
        gb = sb("gb", [P, GB_RING, TOKENS])
        hg = sb("hg", [P, H_RING, TOKENS])
        hh, hl = sb("hh", [P, H_RING, TOKENS], F32R), sb("hl", [P, H_RING, TOKENS], F32R)
        yT = sb("yT", [P, TOKENS])
        nat_h, nat_l = sb("nat_h", [P, 2, TOKENS], F32R), sb("nat_l", [P, 2, TOKENS], F32R)
        qs, ks = sb("qs", [KROWS, HEADS, TOKENS], F32R), sb("ks", [KROWS, HEADS, TOKENS], F32R)
        V = sb("V", [P, TILES, HD])
        neg_m = sb("neg_m", [P, TILES, HEADS])
        mrow_h, mrow_l = sb("mrow_h", [HEADS, TOKENS], F32R), sb("mrow_l", [HEADS, TOKENS], F32R)
        probs = sb("probs", [P, P_RING, GROUP, TOKENS])
        psums = sb("psums", [P, GROUP, TOKENS])
        rden, o_n = sb("rden", [P, TOKENS]), sb("o_n", [P, TOKENS])
        o_h, o_l = sb("o_h", [P, GROUPS, TOKENS], F32R), sb("o_l", [P, GROUPS, TOKENS], F32R)
        w1_raw = probs[:, 0, :, :].rearrange("p a n -> p (a n)")
        w2_raw = probs[:, 1, :, :].rearrange("p a n -> p (a n)").rearrange("p (u d) -> p u d", u=UNITS)
        wq_raw = psums[:, 0, 0:GROUPS * D].rearrange("p (g d) -> p g d", g=GROUPS)
        wo_raw = psums[:, 0, 256:256 + HD]
        wk_raw = psums[:, 1, 0:GROUPS * RANK].rearrange("p (g r) -> p g r", g=GROUPS)
        wv_raw = psums[:, 1, 128:128 + GROUPS * RANK].rearrange("p (g r) -> p g r", g=GROUPS)
        down_raw = psums[0:RANK, 1, 256:256 + D]
        gw_raw = psums[0:EXPERTS, 2, 0:D]
        b1_raw = psums[0:UNITS, 2, 128:128 + P]

        dve_ring = [ctx.enter_context(nc.psum_tensor(f"dve_ring{i}", [P, TOKENS], F32)) for i in range(D_RING)]
        act_ring = [ctx.enter_context(nc.psum_tensor(f"act_ring{i}", [P, TOKENS], F32)) for i in range(A_RING)]
        y_bank = ctx.enter_context(nc.psum_tensor("y_bank", [P, TOKENS], F32))
        o_bank = ctx.enter_context(nc.psum_tensor("o_bank", [P, TOKENS], F32))

        S = {name: sem(name) for name in ADDS}
        d_full, d_done, a_full, a_done = S["d_full"], S["d_done"], S["a_full"], S["a_done"]
        weights_in = sem("weights_in")
        consts_made = sem("consts_made")
        setup_pe = sem("setup_pe")
        setup_dve = sem("setup_dve")
        link = sem("link")
        pool_link = sem("pool_link")

        class At:

            def __init__(self, step, turn):
                self.stage, _, self.name, self.k = self.step = step
                self.turn = turn
                self.batch = step[1] if turn is None else turn + LOOP0

            def count(self, name, step=None, k=None, back=0):
                key = (self.stage, self.step[1], step or self.name, self.k if k is None else k)
                n = counts[name, key] - back
                return n if self.turn is None else n + self.turn * per_body[name]

            def bank(self, name, ring):
                n = counts[name, self.step] - ADDS[name][self.name]
                return n % ring

        def wait(eng, semaphore, value):
            if isinstance(value, int) and value <= 0:
                return
            eng.wait_ge(semaphore, value)

        def walk(eng, does):
            for step in first:
                if step[2] in does:
                    does[step[2]](At(step, None))
            with eng.Fori(0, LOOPS) as turn:
                for step in body:
                    if step[2] in does:
                        does[step[2]](At(step, turn))
            for step in last:
                if step[2] in does:
                    does[step[2]](At(step, None))

        block = ctx.enter_context(nc.Block())

        @block.sync
        def _(sp):
            x_v = x.rearrange("b (p n) d -> b p n d", n=TILES)
            out_v = out.rearrange("b (p n) d -> b p n d", n=TILES)

            sp.dma_start(x_of["in"][:], x_v[0]).then_inc(S["x_in"], 16)
            for dst, src in (
                (wq_raw, wq.rearrange("(g p) d -> p g d", p=P)), (wo_raw, wo),
                (wk_raw, wk_up.rearrange("(g p) r -> p g r", p=P)),
                (wv_raw, wv_up.rearrange("(g p) r -> p g r", p=P)),
                (down_raw, wkv_down), (gw_raw, gate_w),
                (b1_raw, b1.rearrange("e (h p) -> (e h) p", p=P)),
                (w2_raw, w2.rearrange("e (h p) d -> p (e h) d", p=P)),
                (w1_raw.rearrange("p (e h) -> p e h", e=EXPERTS), w1.rearrange("e p h -> p e h")),
                (b2_sb[:], b2),
            ) + tuple((gate_bias[:, n, :], gate_b.partition_broadcast(P)) for n in range(TILES)):
                sp.dma_start(dst, src).then_inc(weights_in, 16)

            def load(at):
                if at.turn is None and at.batch == BATCHES - 1:
                    return
                sp.wait_ge(d_done, at.count("d_done", "back"))
                sp.dma_start(x_of["in"][:], x_v[at.batch + 1]).then_inc(S["x_in"], 16)

            def qk(at):
                sp.wait_ge(d_done, at.count("d_done"))
                kind, g = "qk".index(at.name), at.k
                stack = (qs, ks)[kind]
                halves = ((nat_h, nat_h, nat_l), (nat_h, nat_l, nat_h))[kind]
                for j in range(GROUP):
                    for r, half in enumerate(halves):
                        sp.dma_start(stack[r * DH:(r + 1) * DH, g * GROUP + j, :].bitcast(F32),
                                     half[j * DH:(j + 1) * DH, kind, :].bitcast(F32)).then_inc(S[at.name + "_stacked"], 16)

            def mrow(at):
                sp.wait_ge(d_done, at.count("d_done"))
                for r, row in enumerate((mrow_h, mrow_l)):
                    sp.dma_start(qs[STACK + r:STACK + r + 1, :, :].rearrange("p h n -> p (h n)").bitcast(F32),
                                 row[:].bitcast(F32)).then_inc(S["m_stacked"], 16)

            def store(at):
                sp.wait_ge(d_done, at.count("d_done", "back", 0))
                sp.dma_start(out_v[at.batch], x_of["C"][:]).then_inc(S["x_out"], 16)

            walk(sp, {"load": load, "q": qk, "k": qk, "mrow": mrow, "store": store})
            sp.wait_ge(S["x_out"], 16 * BATCHES)

        WEIGHT_DMAS = 10 + TILES

        @block.gpsimd
        def _(pool):
            pool.memset(ident[:], 0.0).then_inc(pool_link, 1)
            pool.memset(pick_f[:], 0.0).then_inc(pool_link, 1)
            pool.memset(ones[:], 1.0)
            for e in range(EXPERTS):
                pool.memset(first_wins[:, :, e:e + 1], float(EXPERTS - e))
            pool.wait_ge(pool_link, 2)
            pool.affine_select(out=ident[:], in_=ident[:], compare_op=ALU.not_equal, fill=1.0, base=0,
                               pattern=[[-1, P]], channel_multiplier=1)
            pool.affine_select(out=pick_f[:], in_=pick_f[:], compare_op=ALU.not_equal, fill=1.0, base=0,
                               pattern=[[-1, EXPERTS], [0, P]], channel_multiplier=1).then_inc(pool_link, 1)
            pool.wait_ge(pool_link, 3)
            pool.affine_select(out=pick_f[:], in_=pick_f[:], compare_op=ALU.not_equal, fill=1.0, base=-64,
                               pattern=[[-1, EXPERTS], [0, P]], channel_multiplier=1).then_inc(consts_made, 1)

            def h(at):
                slot = at.k % H_RING
                pool.wait_ge(S["hh_done"], at.count("hh_done"))
                pool.tensor_tensor(hl[:, slot, :], hg[:, slot, :], hh[:, slot, :].bitcast(F32),
                                   ALU.subtract).then_inc(S["hl_done"], 1)

            def add(at):
                g, kt = divmod(at.k, TILES)
                pool.wait_ge(a_done, at.count("a_done", "s", at.k * GROUP + GROUP - 1))
                slot, before = at.k % P_RING, (at.k - 1) % P_RING
                if kt == 1:
                    wait(pool, d_full, sums_before(at))
                    first_term = probs[:, before, :, :]
                else:
                    pool.wait_ge(S["p_added"], at.count("p_added", back=1))
                    first_term = psums[:]
                pool.tensor_tensor(psums[:], first_term, probs[:, slot, :, :], ALU.add).then_inc(S["p_added"], 1)

            def sums_before(at):
                if at.k >= TILES:
                    return at.count("d_full", "sum", 0)
                if at.turn is None and at.batch == 0:
                    return 0
                return at.count("d_full", "sum", GROUPS - 1, back=per_body["d_full"])

            walk(pool, {"h": h, "add": add})

        @block.scalar
        def _(act):
            def logits(at):
                act.wait_ge(S["lg_done"], at.count("lg_done"))
                act.activation(ex[:], lg[:], ACT.Exp).then_inc(S["ex_done"], 1)

            def gb_(at):
                act.wait_ge(a_full, at.count("a_full"))
                if at.k >= GB_RING:
                    act.wait_ge(d_done, at.count("d_done", "h", 2 * (at.k - GB_RING) + 1))
                act.activation(gb[:, at.k % GB_RING, :], act_ring[at.bank("a_full", A_RING)][:],
                               ACT.Copy).then_inc(a_done, 1)

            def h(at):
                slot = at.k % H_RING
                act.wait_ge(d_done, at.count("d_done"))
                wait(act, S["y_used"], at.count("y_used", "y", at.k, back=H_RING))
                act.activation(hh[:, slot, :], hg[:, slot, :], ACT.Copy).then_inc(S["hh_done"], 1)

            def fix(at):
                act.wait_ge(S["y_full"], at.count("y_full"))
                act.activation(yT[:], y_bank[:], ACT.Copy).then_inc(S["yT_done"], 1)

            def v(at):
                act.wait_ge(a_full, at.count("a_full"))
                act.activation(V[:, 2 * at.k:2 * at.k + 2, :].rearrange("p n d -> p (n d)"),
                               act_ring[at.bank("a_full", A_RING)][:], ACT.Copy).then_inc(a_done, 1)

            def s_(at):
                m, j = divmod(at.k, GROUP)
                act.wait_ge(a_full, at.count("a_full"))
                if j == 0:
                    wait(act, S["p_used"], at.count("p_used", "pv", m, back=P_RING))
                    g, kt = divmod(m, TILES)
                    if kt >= 2:
                        act.wait_ge(S["p_added"], at.count("p_added", "add", g * TILES + (1 if kt == 2 else kt - 2)))
                    else:
                        wait(act, S["p_added"], at.count("p_added", "add", g * TILES + 1, back=2 - kt))
                act.activation(probs[:, m % P_RING, j, :], act_ring[at.bank("a_full", A_RING)][:],
                               ACT.Exp, scale=SCALE).then_inc(a_done, 1)

            def wo_(at):
                act.wait_ge(a_full, at.count("a_full"))
                act.activation(yT[:], act_ring[at.bank("a_full", A_RING)][:], ACT.Copy).then_inc(a_done, 1)

            act.wait_ge(weights_in, 16 * WEIGHT_DMAS)
            walk(act, {"logits": logits, "gb": gb_, "h": h, "fix": fix, "v": v, "s": s_, "wo": wo_})

        @block.vector
        def _(dve):
            V_ = nc.vector
            steps_linked = {"norm": 5 + 3 * NEWTON_STEPS, "logits": 16, "gT": 1, "xT": 1, "mrow": 1, "sum": 1, "q": 1, "k": 1}
            per_turn = sum(steps_linked.get(st[2], 0) for st in body)
            linked = {"n": 0, "turn": None}

            def chain(ins):
                linked["n"] += 1
                ins.then_inc(link, 1)
                n, turn = linked["n"], linked["turn"]
                dve.wait_ge(link, n if turn is None else n + turn * per_turn)

            def split_done(hi, lo, src):
                chain(V_.tensor_copy(hi, src))
                return V_.tensor_tensor(lo, src, hi.bitcast(F32), ALU.subtract)

            V_.memset(corr[:].bitcast(F32), 0.0)
            V_.memset(gT[:].bitcast(F32), 0.0)
            V_.memset(b1_masked[:], 0.0)
            V_.memset(ks[STACK:KROWS, :, :].bitcast(F32), 1.0)
            dve.wait_ge(weights_in, 16 * WEIGHT_DMAS)
            split_done(w1h[:], w1l[:], w1_raw)
            split_done(w2h[:], w2l[:], w2_raw)
            dve.wait_ge(consts_made, 1)
            V_.tensor_copy(pick[:], pick_f[:])
            dve.wait_ge(setup_pe, 1)
            split_done(wqkv_h[:, 0, :], wqkv_l[:, 0, :], dve_ring[0][:, 0:HD])
            split_done(wo_h[:].rearrange("p g d -> p (g d)"), wo_l[:].rearrange("p g d -> p (g d)"),
                       dve_ring[0][:, HD:HD + GROUPS * D])
            V_.tensor_copy(up_T[:], dve_ring[1][0:RANK, :])
            split_done(gw_h[:], gw_l[:], dve_ring[2][:, 0:EXPERTS])
            for e in range(EXPERTS):
                V_.tensor_copy(b1_masked[:, 2 * e:2 * e + 2, e], dve_ring[2][:, EXPERTS + 2 * e:EXPERTS + 2 * e + 2])
            V_.tensor_scalar(neg_b1[:], dve_ring[2][:, EXPERTS:EXPERTS + UNITS], -1.0, None,
                             ALU.mult).then_inc(setup_dve, 1)
            dve.wait_ge(setup_pe, 2)
            split_done(wqkv_h[:, 1:3, :].rearrange("p a n -> p (a n)"),
                       wqkv_l[:, 1:3, :].rearrange("p a n -> p (a n)"), act_ring[0][:])
            chain(V_.tensor_tensor(corr_f[:], act_ring[1][0:EXPERTS, 0:D], b2_sb[:], ALU.add))
            chain(V_.tensor_copy(corr[0:EXPERTS, :], corr_f[:]))
            V_.tensor_copy(corr[64:64 + EXPERTS, :], corr[0:EXPERTS, :])
            V_.tensor_tensor(corr[32:32 + EXPERTS, :], corr_f[:], corr[0:EXPERTS, :].bitcast(F32),
                             ALU.subtract).then_inc(setup_dve, 1)

            def norm(at):
                xb = x_before[at.stage]
                if at.stage == "A":
                    dve.wait_ge(S["x_in"], at.batch * 16 + 16)
                else:
                    prev = counts["d_done", ("AB"["BC".index(at.stage)], at.step[1], "back", 0)]
                    dve.wait_ge(d_done, prev if at.turn is None else prev + at.turn * per_body["d_done"])
                for n in range(TILES):
                    last = V_.bn_stats(out=stats[:, n, :], in_=xb[:, n, :])
                chain(last)
                V_.memset(nt[:, 0:1], 0.0)
                for n in range(TILES):
                    last = V_.bn_aggr(mv[:, n, :], stats[:, n, :])
                chain(last)
                chain(V_.tensor_scalar(veps[:], mv[:, :, 1], EPS, None, ALU.add))
                chain(V_.tensor_scalar(half_bits[:], veps[:].bitcast(I32), 1, None, ALU.logical_shift_right))
                last = V_.tensor_scalar(rstd[:].bitcast(I32), half_bits[:], -1.0, float(RSQRT_MAGIC), ALU.mult, ALU.add)
                for _ in range(NEWTON_STEPS):
                    chain(last)
                    chain(V_.tensor_tensor(nt[:], rstd[:], rstd[:], ALU.mult))
                    chain(V_.scalar_tensor_tensor(out=nt[:], in0=nt[:], scalar=-0.5, in1=veps[:], op0=ALU.mult, op1=ALU.mult))
                    last = V_.scalar_tensor_tensor(out=rstd[:], in0=nt[:], scalar=1.5, in1=rstd[:], op0=ALU.add, op1=ALU.mult)
                chain(last)
                for n in range(TILES):
                    last = V_.tensor_scalar(xn[:, n, :], xb[:, n, :], mv[:, n, 0:1], rstd[:, n:n + 1],
                                            ALU.subtract, ALU.mult)
                last.then_inc(S["xn_done"], 1)

            def ring(at):
                dve.wait_ge(d_full, at.count("d_full"))
                return dve_ring[at.bank("d_full", D_RING)]

            def xT(at):
                split_done(xT_h[:], xT_l[:], ring(at)[:]).then_inc(d_done, 1)

            def wide(small):
                return small.unsqueeze(2).to_broadcast([P, TILES, EXPERTS])

            def logits(at):
                bank = ring(at)
                V_.tensor_tensor(lg[:], bank[:, 0:TILES * EXPERTS].rearrange("p (n e) -> p n e", n=TILES),
                                 gate_bias[:], ALU.add).then_inc(d_done, 2)
                dve.wait_ge(d_done, at.count("d_done"))
                chain(V_.tensor_reduce(mx[:], lg[:], AX.X, ALU.max))
                V_.tensor_tensor(lg[:], lg[:], wide(mx[:]), ALU.subtract).then_inc(S["lg_done"], 1)
                dve.wait_ge(S["ex_done"], at.count("ex_done"))
                chain(V_.tensor_reduce(sm[:], ex[:], AX.X, ALU.add))
                chain(V_.reciprocal(rs[:], sm[:]))
                chain(V_.tensor_tensor(pr[:], ex[:], wide(rs[:]), ALU.mult))
                chain(V_.tensor_reduce(m1[:], pr[:], AX.X, ALU.max))
                chain(V_.tensor_tensor(eq[:], pr[:], wide(m1[:]), ALU.is_equal))
                chain(V_.tensor_tensor(cand[:], eq[:], first_wins[:], ALU.mult))
                chain(V_.tensor_reduce(s1[:], cand[:], AX.X, ALU.max))
                chain(V_.tensor_tensor(one1[:], cand[:], wide(s1[:]), ALU.is_equal))
                chain(V_.scalar_tensor_tensor(out=pr2[:], in0=one1[:], scalar=-2.0, in1=pr[:], op0=ALU.mult, op1=ALU.add))
                chain(V_.tensor_reduce(m2[:], pr2[:], AX.X, ALU.max))
                chain(V_.tensor_tensor(eq[:], pr2[:], wide(m2[:]), ALU.is_equal))
                chain(V_.tensor_tensor(cand[:], eq[:], first_wins[:], ALU.mult))
                chain(V_.tensor_reduce(s2[:], cand[:], AX.X, ALU.max))
                chain(V_.tensor_tensor(one2[:], cand[:], wide(s2[:]), ALU.is_equal))
                chain(V_.tensor_tensor(one2[:], one2[:], one1[:], ALU.add))
                V_.scalar_tensor_tensor(out=G[:], in0=pr[:], scalar=0.5, in1=one2[:], op0=ALU.mult,
                                        op1=ALU.mult).then_inc(S["g_done"], 1)

            def gT_(at):
                bank = ring(at)
                chain(V_.tensor_copy(gT[0:EXPERTS, :], bank[0:EXPERTS, :]))
                V_.tensor_copy(gT[32:32 + EXPERTS, :], gT[0:EXPERTS, :])
                V_.tensor_tensor(gT[64:64 + EXPERTS, :], bank[0:EXPERTS, :], gT[0:EXPERTS, :].bitcast(F32),
                                 ALU.subtract).then_inc(d_done, 1)

            def h(at):
                wait(dve, S["hl_done"], at.count("hl_done", back=H_RING))
                if at.k % 2 == 0:
                    dve.wait_ge(a_done, at.count("a_done", "gb", at.k // 2))
                V_.scalar_tensor_tensor(out=hg[:, at.k % H_RING, :], in0=ring(at)[:], scalar=neg_b1[:, at.k:at.k + 1],
                                        in1=gb[:, (at.k // 2) % GB_RING, :], op0=ALU.max, op1=ALU.mult).then_inc(d_done, 1)

            def back(at):
                if at.stage == "C":
                    wait(dve, S["x_out"], at.count("x_out", "store", back=16))
                V_.tensor_tensor(x_of[at.stage][:].rearrange("p n d -> p (n d)"), ring(at)[:],
                                 x_before[at.stage][:].rearrange("p n d -> p (n d)"), ALU.add).then_inc(d_done, 1)

            def qk(at):
                slot, stacked = "qk".index(at.name), at.name + "_stacked"
                wait(dve, S[stacked], at.count(stacked, back=ADDS[stacked][at.name]))
                split_done(nat_h[:, slot, :], nat_l[:, slot, :], ring(at)[:]).then_inc(d_done, 1)

            def max_(at):
                head, n = divmod(at.k, TILES)
                V_.tensor_reduce(neg_m[:, n, head:head + 1], ring(at)[:], AX.X, ALU.max, negate=True).then_inc(d_done, 1)

            def mrow(at):
                bank = ring(at)
                split_done(mrow_h[:], mrow_l[:], bank[0:HEADS, :]).then_inc(d_done, 2)

            def sum_(at):
                g = at.k
                V_.reciprocal(rden[:], ring(at)[:]).then_inc(d_done, 1)
                dve.wait_ge(d_done, at.count("d_done"))
                V_.tensor_tensor(o_n[:], o_bank[:], rden[:], ALU.mult).then_inc(S["o_read"], 1)
                dve.wait_ge(S["o_read"], at.count("o_read", "onorm", g))
                chain(V_.tensor_copy(o_h[:, g, :], o_n[:]))
                V_.tensor_tensor(o_l[:, g, :], o_n[:], o_h[:, g, :].bitcast(F32), ALU.subtract).then_inc(S["o_done"], 1)

            does = {"norm": norm, "xT": xT, "logits": logits, "gT": gT_, "h": h, "back": back, "q": qk, "k": qk,
                    "max": max_, "mrow": mrow, "sum": sum_}
            for step in first:
                if step[2] in does:
                    does[step[2]](At(step, None))
            with dve.Fori(0, LOOPS) as turn:
                linked["turn"] = turn
                before = linked["n"]
                for step in body:
                    if step[2] in does:
                        does[step[2]](At(step, turn))
                assert linked["n"] - before == per_turn, (linked["n"] - before, per_turn)
            linked["n"] += (LOOPS - 1) * per_turn
            linked["turn"] = None
            for step in last:
                if step[2] in does:
                    does[step[2]](At(step, None))

        @block.tensor
        def _(pe):
            def product3(dst, wh, wl, mh, ml, start=True, stop=True):
                pe_mm(dst, wh, mh, start=start, stop=False)
                pe_mm(dst, wl, mh, start=False, stop=False)
                return pe_mm(dst, wh, ml, start=False, stop=stop)

            def pe_mm(dst, w, m, start=True, stop=True):
                return nc.tensor.matmul(dst, w, m, start=start, stop=stop)

            pe.wait_ge(weights_in, 16 * WEIGHT_DMAS)
            pe.wait_ge(consts_made, 1)
            for g in range(GROUPS):
                nc.tensor.transpose(dve_ring[0][:, g * P:(g + 1) * P], wq_raw[:, g, :], ident[:])
                nc.tensor.transpose(dve_ring[0][:, HD + g * D:HD + (g + 1) * D], wo_raw[:, g * P:(g + 1) * P], ident[:])
                nc.tensor.transpose(dve_ring[1][0:RANK, g * P:(g + 1) * P], wk_raw[:, g, :], ident[:])
                nc.tensor.transpose(dve_ring[1][0:RANK, HD + g * P:HD + (g + 1) * P], wv_raw[:, g, :], ident[:])
            nc.tensor.transpose(dve_ring[2][:, 0:EXPERTS], gw_raw, ident[0:EXPERTS, 0:EXPERTS])
            nc.tensor.transpose(dve_ring[2][:, EXPERTS:EXPERTS + UNITS], b1_raw,
                                ident[0:UNITS, 0:UNITS]).then_inc(setup_pe, 1)
            pe.wait_ge(setup_dve, 1)
            pe_mm(act_ring[0][:], down_raw, up_T[:])
            for u in range(UNITS):
                last = pe_mm(act_ring[1][0:EXPERTS, 0:D], b1_masked[:, u, :], w2_raw[:, u, :],
                             start=(u == 0), stop=(u == UNITS - 1))
            last.then_inc(setup_pe, 1)
            pe.wait_ge(setup_dve, 2)

            def ring_d(at):
                wait(pe, d_done, at.count("d_done", back=D_RING + ADDS["d_full"][at.name] - 1))
                return dve_ring[at.bank("d_full", D_RING)]

            def ring_a(at):
                wait(pe, a_done, at.count("a_done", back=A_RING))
                return act_ring[at.bank("a_full", A_RING)]

            def tokens(n):
                return slice(n * P, (n + 1) * P)

            def xT(at):
                bank = ring_d(at)
                pe.wait_ge(S["xn_done"], at.count("xn_done", "norm"))
                for n in range(TILES):
                    last = nc.tensor.transpose(bank[:, tokens(n)], xn[:, n, :], ident[:])
                last.then_inc(d_full, 1)

            def logits(at):
                bank = ring_d(at)
                pe.wait_ge(d_done, at.count("d_done", "xT", 0))
                for n in range(TILES):
                    last = product3(bank[:, n * EXPERTS:(n + 1) * EXPERTS], xT_h[:, tokens(n)], xT_l[:, tokens(n)],
                                    gw_h[:], gw_l[:])
                last.then_inc(d_full, 2)

            def gT_(at):
                bank = ring_d(at)
                pe.wait_ge(S["g_done"], at.count("g_done", "logits"))
                for n in range(TILES):
                    last = nc.tensor.transpose(bank[0:EXPERTS, tokens(n)], G[:, n, :], ident[:])
                last.then_inc(d_full, 1)

            def gb_(at):
                bank = ring_a(at)
                if at.k == 0:
                    pe.wait_ge(d_done, at.count("d_done", "gT", 0))
                pe_mm(bank[:], pick[:, at.k, :], gT[:]).then_inc(a_full, 1)

            def h(at):
                product3(ring_d(at)[:], w1h[:, at.k * P:(at.k + 1) * P], w1l[:, at.k * P:(at.k + 1) * P],
                         xT_h[:], xT_l[:]).then_inc(d_full, 1)

            def y(at):
                slot = at.k % H_RING
                pe.wait_ge(S["hl_done"], at.count("hl_done", "h"))
                product3(y_bank[:], w2h[:, at.k, :], w2l[:, at.k, :], hh[:, slot, :], hl[:, slot, :],
                         start=at.k == 0, stop=False).then_inc(S["y_used"], 1)

            def fix(at):
                pe_mm(y_bank[:], corr[:], gT[:], start=False, stop=True).then_inc(S["y_full"], 1)

            def back(at):
                bank = ring_d(at)
                if at.stage == "B":
                    pe.wait_ge(a_done, at.count("a_done", "wo"))
                else:
                    pe.wait_ge(S["yT_done"], at.count("yT_done", "fix"))
                for n in range(TILES):
                    last = nc.tensor.transpose(bank[:, tokens(n)], yT[:, tokens(n)], ident[:])
                last.then_inc(d_full, 1)

            def qk(at):
                bank, kind, g = ring_d(at), "qk".index(at.name), at.k
                if at.k == 0:
                    pe.wait_ge(d_done, at.count("d_done", "xT", 0))
                product3(bank[:], wqkv_h[:, kind, g * P:(g + 1) * P], wqkv_l[:, kind, g * P:(g + 1) * P],
                         xT_h[:], xT_l[:]).then_inc(d_full, 1)

            def v(at):
                bank = ring_a(at)
                for i in range(2):
                    n = 2 * at.k + i
                    last = product3(bank[:, i * HD:(i + 1) * HD], xT_h[:, tokens(n)], xT_l[:, tokens(n)],
                                    wqkv_h[:, 2, :], wqkv_l[:, 2, :])
                last.then_inc(a_full, 1)

            def max_(at):
                head, n = divmod(at.k, TILES)
                bank = ring_d(at)
                if at.k == 0:
                    pe.wait_ge(S["q_stacked"], at.count("q_stacked", "q", GROUPS - 1))
                    pe.wait_ge(S["k_stacked"], at.count("k_stacked", "k", GROUPS - 1))
                pe_mm(bank[:], qs[0:STACK, head, tokens(n)], ks[0:STACK, head, :]).then_inc(d_full, 1)

            def mrow(at):
                bank = ring_d(at)
                pe.wait_ge(d_done, at.count("d_done", "max", HEADS * TILES - 1))
                for n in range(TILES):
                    last = nc.tensor.transpose(bank[0:HEADS, tokens(n)], neg_m[:, n, :], ident[:])
                last.then_inc(d_full, 2)

            def s_(at):
                m, j = divmod(at.k, GROUP)
                g, kt = divmod(m, TILES)
                bank = ring_a(at)
                if at.k == 0:
                    pe.wait_ge(S["m_stacked"], at.count("m_stacked", "mrow", 0))
                head = g * GROUP + j
                pe_mm(bank[:], ks[:, head, tokens(kt)], qs[:, head, :]).then_inc(a_full, 1)

            def pv(at):
                g, kt = divmod(at.k, TILES)
                pe.wait_ge(a_done, at.count("a_done", "s", at.k * GROUP + GROUP - 1))
                if kt == 0:
                    wait(pe, S["o_read"], at.count("o_read", "onorm", g, back=1))
                for j in range(GROUP):
                    head = g * GROUP + j
                    last = nc.tensor.matmul(o_bank[j * DH:(j + 1) * DH, :], V[:, kt, head * DH:(head + 1) * DH],
                                            probs[:, at.k % P_RING, j, :], start=kt == 0, stop=kt == TILES - 1)
                last.then_inc(S["p_used"], 1)

            def sum_(at):
                bank = ring_d(at)
                pe.wait_ge(S["p_added"], at.count("p_added", "add", at.k * TILES + TILES - 1))
                for j in range(GROUP):
                    last = nc.tensor.matmul(bank[j * DH:(j + 1) * DH, :], ones[:], psums[:, j, :], start=True, stop=True)
                last.then_inc(d_full, 1)

            def wo_(at):
                bank = ring_a(at)
                pe.wait_ge(S["o_done"], at.count("o_done", "onorm", GROUPS - 1))
                for g in range(GROUPS):
                    last = product3(bank[:], wo_h[:, g, :], wo_l[:, g, :], o_h[:, g, :], o_l[:, g, :],
                                    start=g == 0, stop=g == GROUPS - 1)
                last.then_inc(a_full, 1)

            walk(pe, {"xT": xT, "logits": logits, "gT": gT_, "gb": gb_, "h": h, "y": y, "fix": fix, "back": back,
                      "q": qk, "k": qk, "v": v, "max": max_, "mrow": mrow, "s": s_, "pv": pv, "sum": sum_, "wo": wo_})


_INS = ['L0_attn_x', 'L0_attn_Wq', 'L0_attn_Wkv_down', 'L0_attn_Wk_up', 'L0_attn_Wv_up', 'L0_attn_Wo',
        'L0_ffn_gate_w', 'L0_ffn_gate_b', 'L0_ffn_w1', 'L0_ffn_b1', 'L0_ffn_w2', 'L0_ffn_b2']


def kernel(**inputs):
    import numpy as _np
    import concourse.bacc as _bacc
    from concourse import mybir as _mybir
    from concourse.bass_utils import run_bass_kernel_spmd as _run

    nc = _bacc.Bacc("TRN2", target_bir_lowering=False, num_devices=1)
    arrays, args = {}, []
    for name in _INS:
        a = _np.ascontiguousarray(inputs[name])
        arrays[f"in_{name}_dram"] = a
        args.append(nc.dram_tensor(f"in_{name}_dram", a.shape, _mybir.dt.from_np(a.dtype), kind="ExternalInput").ap())
    shape = inputs['L0_attn_x'].shape
    args.append(nc.dram_tensor("out_0_dram", shape, _mybir.dt.float32, kind="ExternalOutput").ap())
    macaron_kernel(nc, *args)
    r = _run(nc, [arrays], core_ids=[0])
    return r.results[0]["out_0_dram"]
```

```python
from contextlib import ExitStack

import concourse.bass as bass
from concourse import mybir
from concourse.alu_op_type import AluOpType as ALU

F32 = mybir.dt.float32
F32R = mybir.dt.float32r
I32 = mybir.dt.int32
ACT = mybir.ActivationFunctionType
AX = mybir.AxisListType

P = 128
EPS = 1e-5
RSQRT_MAGIC = 0x5F3759DF
NEWTON_STEPS = 3

EXPERTS, UNITS = 8, 16
TILES, HEADS, GROUP = 4, 8, 4
GROUPS = HEADS // GROUP
LAG = 3




def turn_steps(t, batches):
    slots = [[] for _ in range(2 * UNITS)]

    def put(slot, stage, batch, name, k=0):
        if 0 <= batch < batches:
            slots[slot].append((stage, batch, name, k))

    for half, stage, b in ((0, "A", t), (UNITS, "C", t - 2)):
        for u in range(UNITS):
            if u % 2 == 0 and u // 2 + 1 < EXPERTS:
                put(half + u, stage, b, "gb", u // 2 + 1)
            put(half + u, stage, b, "h", u)
            if u >= LAG:
                put(half + u, stage, b, "y", u - LAG)
    for half, stage, b in ((UNITS, "A", t), (0, "C", t - 3)):
        for i in range(LAG):
            put(half + i, stage, b, "y", UNITS - LAG + i)
        put(half + LAG - 1, stage, b, "fix")
        put(half + 5, stage, b, "back")
    put(6, "C", t - 3, "store")
    put(UNITS + 5, "A", t + 1, "load")
    b = t - 1
    for n in range(2):
        put(2 + n, "B", b, "v", n)
    for n in range(HEADS * TILES):
        put(n // 2, "B", b, "max", n)
    put(10, "B", b, "mrow", 0)
    put(UNITS + 2, "B", b, "mrow", 1)
    for n in range(HEADS * TILES):
        put(UNITS + n // 2, "B", b, "s", n)
    late = [(3, "pv", 0), (5, "pv", 1), (7, "pv", 2), (9, "pv", 3), (12, "sum", 0), (13, "pv", 4), (14, "pv", 5),
            (15, "pv", 6), (17, "pv", 7), (21, "sum", 1), (23, "wo", 0), (24, "back", 0)]
    for g, start in enumerate((5, 15)):
        for kt in range(1, TILES):
            late += [(start + 2 * (kt - 1) + j // 2, "add", (g * TILES + kt) * GROUP + j) for j in range(GROUP)]
    for at, name, k in late:
        if at < UNITS:
            put(UNITS + at, "B", b, name, k)
        else:
            put(at - UNITS, "B", b - 1, name, k)
    for at, stage, b in ((8, "C", t - 2), (UNITS + 8, "A", t + 1)):
        put(at, stage, b, "norm")
        put(at + 2, stage, b, "xT")
        put(at + 4, stage, b, "logits")
        put(at + 6, stage, b, "gT")
        put(at + 7, stage, b, "gb", 0)
    put(UNITS + 6, "B", t, "norm")
    put(UNITS + 8, "B", t, "xT")
    put(UNITS + 9, "B", t, "q", 0)
    put(UNITS + 10, "B", t, "k", 0)
    put(UNITS + 15, "B", t, "q", 1)
    put(0, "B", t - 1, "k", 1)
    return [step for slot in slots for step in slot]


def start_steps():
    return [("A", 0, n, 0) for n in ("load", "norm", "xT", "logits", "gT", "gb")]


ADDS = {
    "d_full": {"xT": 1, "logits": 2, "gT": 1, "h": 1, "back": 1, "q": 1, "k": 1, "max": 1, "mrow": 1, "sum": 1},
    "a_full": {"gb": 1, "v": 1, "s": 1, "wo": 1},
    "xn_done": {"norm": 1},
    "lg_done": {"logits": 1},
    "ex_done": {"logits": 1},
    "g_done": {"logits": 1},
    "hh_done": {"h": 1},
    "hl_done": {"h": 1},
    "y_used": {"y": 1},
    "y_full": {"fix": 1},
    "yT_done": {"fix": 1},
    "q_stacked": {"q": 16 * 3 * GROUP},
    "k_stacked": {"k": 16 * 3 * GROUP},
    "m_stacked": {"mrow": 32},
    "p_used": {"pv": 1},
    "p_added": {"add": 1},
    "o_read": {"sum": 1},
    "o_done": {"sum": 1},
    "x_in": {"load": 16},
    "x_out": {"store": 16},
}
ADDS["d_done"] = ADDS["d_full"]
ADDS["a_done"] = ADDS["a_full"]


def macaron_kernel(nc, x, wq, wkv_down, wk_up, wv_up, wo, gate_w, gate_b, w1, b1, w2, b2, out):
    BATCHES, TOKENS, D = x.shape
    HID = w1.shape[2]
    RANK = wkv_down.shape[0]
    HD = wq.shape[0]
    DH = HD // HEADS
    SCALE = float(DH) ** -0.5
    assert D == P and TOKENS == TILES * P and HID == 2 * P and HD == GROUPS * P and w1.shape[0] == EXPERTS
    STACK = 3 * DH
    KROWS = STACK + 2
    GROWS = 72
    D_RING, A_RING, X_RING = 3, 3, 4
    H_RING, GB_RING, P_RING = 4, 4, TILES

    FIRST_LOOPED, LAST_LOOPED = 3, BATCHES - 2
    LOOPS = LAST_LOOPED - FIRST_LOOPED + 1
    turns = [turn_steps(t, BATCHES) for t in range(BATCHES + 3)]
    before = start_steps() + [st for t in range(FIRST_LOOPED) for st in turns[t]]
    body = turns[FIRST_LOOPED]
    after = [st for t in range(LAST_LOOPED + 1, BATCHES + 3) for st in turns[t]]
    per_body = {sem: sum(adds.get(st[2], 0) for st in body) for sem, adds in ADDS.items()}
    assert per_body["d_full"] % D_RING == 0 and per_body["a_full"] % A_RING == 0
    counts = {}
    for sem, adds in ADDS.items():
        n = 0
        for st in start_steps() + [st for steps in turns for st in steps]:
            n += adds.get(st[2], 0)
            if st[2] in adds:
                counts[sem, st] = n

    with ExitStack() as ctx:
        def sb(name, shape, dt=F32):
            return ctx.enter_context(nc.sbuf_tensor(name, shape, dt))

        def sem(name):
            return ctx.enter_context(nc.semaphore(name))

        X = sb("X", [P, X_RING, TILES, D])
        w1h, w1l = sb("w1h", [P, EXPERTS * HID], F32R), sb("w1l", [P, EXPERTS * HID], F32R)
        w2h, w2l = sb("w2h", [P, UNITS, D], F32R), sb("w2l", [P, UNITS, D], F32R)
        wqkv_h, wqkv_l = sb("wqkv_h", [P, 3, HD], F32R), sb("wqkv_l", [P, 3, HD], F32R)
        wo_h, wo_l = sb("wo_h", [P, GROUPS, D], F32R), sb("wo_l", [P, GROUPS, D], F32R)
        gw_h, gw_l = sb("gw_h", [P, EXPERTS], F32R), sb("gw_l", [P, EXPERTS], F32R)
        neg_b1 = sb("neg_b1", [P, UNITS])
        b1_masked = sb("b1_masked", [P, UNITS, EXPERTS])
        gate_bias = sb("gate_bias", [P, TILES, EXPERTS])
        first_wins = sb("first_wins", [P, TILES, EXPERTS])
        b2_sb = sb("b2_sb", [EXPERTS, D])
        corr_f = sb("corr_f", [EXPERTS, D])
        corr = sb("corr", [GROWS, D], F32R)
        pick = sb("pick", [GROWS, EXPERTS, P], F32R)
        ident = sb("ident", [P, P])
        ones = sb("ones", [P, DH])
        stats, mv = sb("stats", [P, TILES, 6]), sb("mv", [P, TILES, 2])
        veps, rstd, nt = sb("veps", [P, TILES]), sb("rstd", [P, TILES]), sb("nt", [P, TILES])
        half_bits = sb("half_bits", [P, TILES], I32)
        xn = {s: sb("xn" + s, [P, TILES, D]) for s in "ABC"}
        xT_h = {s: sb("xT_h" + s, [P, TOKENS], F32R) for s in "ABC"}
        xT_l = {s: sb("xT_l" + s, [P, TOKENS], F32R) for s in "ABC"}
        lg, ex, pr = (sb(n, [P, TILES, EXPERTS]) for n in ("lg", "ex", "pr"))
        eq, cand, one1, one2, pr2, G = (sb(n, [P, TILES, EXPERTS]) for n in ("eq", "cand", "one1", "one2", "pr2", "G"))
        mx, sm, rs, m1, s1, m2, s2 = (sb(n, [P, TILES]) for n in ("mx", "sm", "rs", "m1", "s1", "m2", "s2"))
        gT = {s: sb("gT" + s, [GROWS, TOKENS], F32R) for s in "AC"}
        gb = sb("gb", [P, GB_RING, TOKENS])
        hg = sb("hg", [P, H_RING, TOKENS])
        hh, hl = sb("hh", [P, H_RING, TOKENS], F32R), sb("hl", [P, H_RING, TOKENS], F32R)
        yT, yT_B = sb("yT", [P, TOKENS]), sb("yT_B", [P, TOKENS])
        nat_h, nat_l = sb("nat_h", [P, 2, TOKENS], F32R), sb("nat_l", [P, 2, TOKENS], F32R)
        qs, ks = sb("qs", [KROWS, HEADS, TOKENS], F32R), sb("ks", [KROWS, HEADS, TOKENS], F32R)
        V = sb("V", [P, TILES, HD])
        neg_m = sb("neg_m", [P, TILES, HEADS])
        mrow_h, mrow_l = sb("mrow_h", [GROUP, TOKENS], F32R), sb("mrow_l", [GROUP, TOKENS], F32R)
        probs = sb("probs", [P, P_RING, GROUP, TOKENS])
        rden, o_n = sb("rden", [P, TOKENS]), sb("o_n", [P, TOKENS])
        o_h, o_l = sb("o_h", [P, GROUPS, TOKENS], F32R), sb("o_l", [P, GROUPS, TOKENS], F32R)
        pick_f = hg[0:GROWS, 0:2, :].rearrange("p a n -> p (a n)").rearrange("p (e n) -> p e n", e=EXPERTS)
        up_T = hg[0:RANK, 2, :]
        w1_raw = probs[:, 0, :, :].rearrange("p a n -> p (a n)")
        w2_raw = probs[:, 1, :, :].rearrange("p a n -> p (a n)").rearrange("p (u d) -> p u d", u=UNITS)
        wq_raw = probs[:, 2, 0, 0:GROUPS * D].rearrange("p (g d) -> p g d", g=GROUPS)
        wo_raw = probs[:, 2, 0, 256:256 + HD]
        wk_raw = probs[:, 2, 1, 0:GROUPS * RANK].rearrange("p (g r) -> p g r", g=GROUPS)
        wv_raw = probs[:, 2, 1, 128:128 + GROUPS * RANK].rearrange("p (g r) -> p g r", g=GROUPS)
        down_raw = probs[0:RANK, 2, 1, 256:256 + D]
        gw_raw = probs[0:EXPERTS, 2, 2, 0:D]
        b1_raw = probs[0:UNITS, 2, 2, 128:128 + P]

        dve_ring = [ctx.enter_context(nc.psum_tensor(f"dve_ring{i}", [P, TOKENS], F32)) for i in range(D_RING)]
        act_ring = [ctx.enter_context(nc.psum_tensor(f"act_ring{i}", [P, TOKENS], F32)) for i in range(A_RING)]
        y_bank = ctx.enter_context(nc.psum_tensor("y_bank", [P, TOKENS], F32))
        o_bank = ctx.enter_context(nc.psum_tensor("o_bank", [P, TOKENS], F32))

        S = {name: sem(name) for name in ADDS}
        d_full, d_done, a_full, a_done = S["d_full"], S["d_done"], S["a_full"], S["a_done"]
        weights_in = sem("weights_in")
        consts_made = sem("consts_made")
        setup_pe = sem("setup_pe")
        setup_dve = sem("setup_dve")
        link = sem("link")
        pool_link = sem("pool_link")

        class At:

            def __init__(self, step, turn):
                self.stage, _, self.name, self.k = self.step = step
                self.turn = turn
                self.batch = step[1] if turn is None else turn + step[1]

            def count(self, name, step=None, k=None, back=0, batch=0, stage=None):
                def key(turn):
                    return (name, (stage or self.stage, self.step[1] + batch + turn, step or self.name,
                                   self.k if k is None else k))
                if self.turn is None:
                    return counts.get(key(0), 0) - back
                n = counts[key(0)] - back
                assert all(counts[key(i)] - back == n + i * per_body[name] for i in range(LOOPS)), (name, self.step)
                return n + self.turn * per_body[name]

            def bank(self, name, ring):
                return (counts[name, self.step] - ADDS[name][self.name]) % ring

        def x_place(eng, at):
            return at.batch % X_RING if at.turn is None else eng.snap(at.batch % X_RING)

        def wait(eng, semaphore, value):
            if isinstance(value, int) and value <= 0:
                return
            eng.wait_ge(semaphore, value)

        def walk(eng, does):
            for step in before:
                if step[2] in does:
                    does[step[2]](At(step, None))
            with eng.Fori(0, LOOPS) as turn:
                for step in body:
                    if step[2] in does:
                        does[step[2]](At(step, turn))
            for step in after:
                if step[2] in does:
                    does[step[2]](At(step, None))

        block = ctx.enter_context(nc.Block())

        @block.sync
        def _(sp):
            x_v = x.rearrange("b (p n) d -> b p n d", n=TILES)
            out_v = out.rearrange("b (p n) d -> b p n d", n=TILES)

            for dst, src in (
                (wq_raw, wq.rearrange("(g p) d -> p g d", p=P)), (wo_raw, wo),
                (wk_raw, wk_up.rearrange("(g p) r -> p g r", p=P)),
                (wv_raw, wv_up.rearrange("(g p) r -> p g r", p=P)),
                (down_raw, wkv_down), (gw_raw, gate_w),
                (b1_raw, b1.rearrange("e (h p) -> (e h) p", p=P)),
                (w2_raw, w2.rearrange("e (h p) d -> p (e h) d", p=P)),
                (w1_raw.rearrange("p (e h) -> p e h", e=EXPERTS), w1.rearrange("e p h -> p e h")),
                (b2_sb[:], b2),
            ) + tuple((gate_bias[:, n, :], gate_b.partition_broadcast(P)) for n in range(TILES)):
                sp.dma_start(dst, src).then_inc(weights_in, 16)

            def load(at):
                place = x_place(sp, at)
                if at.turn is None:
                    wait(sp, S["xn_done"], at.count("xn_done", "norm", batch=-1))
                wait(sp, S["x_out"], at.count("x_out", "store", stage="C", batch=-X_RING))
                sp.dma_start(X[:, place, :, :], x_v[at.batch]).then_inc(S["x_in"], 16)

            def qk(at):
                sp.wait_ge(d_done, at.count("d_done"))
                kind, g = "qk".index(at.name), at.k
                stack = (qs, ks)[kind]
                halves = ((nat_h, nat_h, nat_l), (nat_h, nat_l, nat_h))[kind]
                for j in range(GROUP):
                    for r, half in enumerate(halves):
                        sp.dma_start(stack[r * DH:(r + 1) * DH, g * GROUP + j, :].bitcast(F32),
                                     half[j * DH:(j + 1) * DH, kind, :].bitcast(F32)).then_inc(S[at.name + "_stacked"], 16)

            def mrow(at):
                sp.wait_ge(d_done, at.count("d_done"))
                for r, row in enumerate((mrow_h, mrow_l)):
                    sp.dma_start(qs[STACK + r:STACK + r + 1, at.k * GROUP:(at.k + 1) * GROUP, :].rearrange("p h n -> p (h n)")
                                 .bitcast(F32), row[:].bitcast(F32)).then_inc(S["m_stacked"], 16)

            def store(at):
                place = x_place(sp, at)
                sp.wait_ge(d_done, at.count("d_done", "back", 0))
                sp.dma_start(out_v[at.batch], X[:, place, :, :]).then_inc(S["x_out"], 16)

            walk(sp, {"load": load, "q": qk, "k": qk, "mrow": mrow, "store": store})
            sp.wait_ge(S["x_out"], 16 * BATCHES)

        WEIGHT_DMAS = 10 + TILES

        @block.gpsimd
        def _(pool):
            pool.memset(ident[:], 0.0).then_inc(pool_link, 1)
            pool.memset(pick_f, 0.0).then_inc(pool_link, 1)
            pool.memset(ones[:], 1.0)
            for e in range(EXPERTS):
                pool.memset(first_wins[:, :, e:e + 1], float(EXPERTS - e))
            pool.wait_ge(pool_link, 2)
            pool.affine_select(out=ident[:], in_=ident[:], compare_op=ALU.not_equal, fill=1.0, base=0,
                               pattern=[[-1, P]], channel_multiplier=1)
            pool.affine_select(out=pick_f, in_=pick_f, compare_op=ALU.not_equal, fill=1.0, base=0,
                               pattern=[[-1, EXPERTS], [0, P]], channel_multiplier=1).then_inc(pool_link, 1)
            pool.wait_ge(pool_link, 3)
            pool.affine_select(out=pick_f, in_=pick_f, compare_op=ALU.not_equal, fill=1.0, base=-64,
                               pattern=[[-1, EXPERTS], [0, P]], channel_multiplier=1).then_inc(consts_made, 1)

            def h(at):
                slot = at.k % H_RING
                pool.wait_ge(S["hh_done"], at.count("hh_done"))
                pool.tensor_tensor(hl[:, slot, :], hg[:, slot, :], hh[:, slot, :].bitcast(F32),
                                   ALU.subtract).then_inc(S["hl_done"], 1)

            def add(at):
                m, j = divmod(at.k, GROUP)
                kt = m % TILES
                pool.wait_ge(S["p_used"], at.count("p_used", "pv", m))
                if kt > 1:
                    pool.wait_ge(S["p_added"], at.count("p_added", "add", at.k - GROUP))
                pool.tensor_tensor(probs[:, kt, j, :], probs[:, kt - 1, j, :], probs[:, kt, j, :],
                                   ALU.add).then_inc(S["p_added"], 1)

            walk(pool, {"h": h, "add": add})

        @block.scalar
        def _(act):
            def logits(at):
                act.wait_ge(S["lg_done"], at.count("lg_done"))
                act.activation(ex[:], lg[:], ACT.Exp).then_inc(S["ex_done"], 1)

            def gb_(at):
                act.wait_ge(a_full, at.count("a_full"))
                act.activation(gb[:, at.k % GB_RING, :], act_ring[at.bank("a_full", A_RING)][:],
                               ACT.Copy).then_inc(a_done, 1)

            def h(at):
                slot = at.k % H_RING
                act.wait_ge(d_done, at.count("d_done"))
                wait(act, S["y_used"], at.count("y_used", "y", at.k, back=H_RING))
                act.activation(hh[:, slot, :], hg[:, slot, :], ACT.Copy).then_inc(S["hh_done"], 1)

            def fix(at):
                act.wait_ge(S["y_full"], at.count("y_full"))
                act.activation(yT[:], y_bank[:], ACT.Copy).then_inc(S["yT_done"], 1)

            def v(at):
                act.wait_ge(a_full, at.count("a_full"))
                act.activation(V[:, 2 * at.k:2 * at.k + 2, :].rearrange("p n d -> p (n d)"),
                               act_ring[at.bank("a_full", A_RING)][:], ACT.Copy).then_inc(a_done, 1)

            def s_(at):
                m, j = divmod(at.k, GROUP)
                g, kt = divmod(m, TILES)
                act.wait_ge(a_full, at.count("a_full"))
                if j == 0:
                    last_group = {"k": GROUPS - 1, "batch": -1} if g == 0 else {"k": g - 1}
                    if kt < TILES - 1:
                        last_group["k"] = (last_group["k"] * TILES + kt + 2) * GROUP - 1
                        wait(act, S["p_added"], at.count("p_added", "add", **last_group))
                    else:
                        wait(act, d_full, at.count("d_full", "sum", **last_group))
                act.activation(probs[:, m % P_RING, j, :], act_ring[at.bank("a_full", A_RING)][:],
                               ACT.Exp, scale=SCALE).then_inc(a_done, 1)

            def wo_(at):
                act.wait_ge(a_full, at.count("a_full"))
                act.activation(yT_B[:], act_ring[at.bank("a_full", A_RING)][:], ACT.Copy).then_inc(a_done, 1)

            act.wait_ge(weights_in, 16 * WEIGHT_DMAS)
            walk(act, {"logits": logits, "gb": gb_, "h": h, "fix": fix, "v": v, "s": s_, "wo": wo_})

        @block.vector
        def _(dve):
            V_ = nc.vector
            steps_linked = {"norm": 5 + 3 * NEWTON_STEPS, "logits": 16, "gT": 1, "xT": 1, "mrow": 1, "sum": 1, "q": 1, "k": 1}
            per_turn = sum(steps_linked.get(st[2], 0) for st in body)
            linked = {"n": 0, "turn": None}

            def chain(ins):
                linked["n"] += 1
                ins.then_inc(link, 1)
                n, turn = linked["n"], linked["turn"]
                dve.wait_ge(link, n if turn is None else n + turn * per_turn)

            def split_done(hi, lo, src):
                chain(V_.tensor_copy(hi, src))
                return V_.tensor_tensor(lo, src, hi.bitcast(F32), ALU.subtract)

            V_.memset(corr[:].bitcast(F32), 0.0)
            for s in "AC":
                V_.memset(gT[s][:].bitcast(F32), 0.0)
            V_.memset(b1_masked[:], 0.0)
            V_.memset(ks[STACK:KROWS, :, :].bitcast(F32), 1.0)
            dve.wait_ge(weights_in, 16 * WEIGHT_DMAS)
            split_done(w1h[:], w1l[:], w1_raw)
            split_done(w2h[:], w2l[:], w2_raw)
            dve.wait_ge(consts_made, 1)
            V_.tensor_copy(pick[:], pick_f)
            dve.wait_ge(setup_pe, 1)
            split_done(wqkv_h[:, 0, :], wqkv_l[:, 0, :], dve_ring[0][:, 0:HD])
            split_done(wo_h[:].rearrange("p g d -> p (g d)"), wo_l[:].rearrange("p g d -> p (g d)"),
                       dve_ring[0][:, HD:HD + GROUPS * D])
            V_.tensor_copy(up_T, dve_ring[1][0:RANK, :])
            split_done(gw_h[:], gw_l[:], dve_ring[2][:, 0:EXPERTS])
            for e in range(EXPERTS):
                V_.tensor_copy(b1_masked[:, 2 * e:2 * e + 2, e], dve_ring[2][:, EXPERTS + 2 * e:EXPERTS + 2 * e + 2])
            V_.tensor_scalar(neg_b1[:], dve_ring[2][:, EXPERTS:EXPERTS + UNITS], -1.0, None,
                             ALU.mult).then_inc(setup_dve, 1)
            dve.wait_ge(setup_pe, 2)
            split_done(wqkv_h[:, 1:3, :].rearrange("p a n -> p (a n)"),
                       wqkv_l[:, 1:3, :].rearrange("p a n -> p (a n)"), act_ring[0][:])
            chain(V_.tensor_tensor(corr_f[:], act_ring[1][0:EXPERTS, 0:D], b2_sb[:], ALU.add))
            chain(V_.tensor_copy(corr[0:EXPERTS, :], corr_f[:]))
            V_.tensor_copy(corr[64:64 + EXPERTS, :], corr[0:EXPERTS, :])
            V_.tensor_tensor(corr[32:32 + EXPERTS, :], corr_f[:], corr[0:EXPERTS, :].bitcast(F32),
                             ALU.subtract).then_inc(setup_dve, 1)

            def norm(at):
                xb = X[:, x_place(dve, at), :, :]
                if at.stage == "A":
                    dve.wait_ge(S["x_in"], at.batch * 16 + 16)
                else:
                    dve.wait_ge(d_done, at.count("d_done", "back", stage="AB"["BC".index(at.stage)]))
                V_.memset(nt[:, 0:1], 0.0)
                for n in range(TILES):
                    last = V_.bn_stats(out=stats[:, n, :], in_=xb[:, n, :])
                chain(last)
                V_.memset(nt[:, 0:1], 0.0)
                for n in range(TILES):
                    last = V_.bn_aggr(mv[:, n, :], stats[:, n, :])
                chain(last)
                chain(V_.tensor_scalar(veps[:], mv[:, :, 1], EPS, None, ALU.add))
                chain(V_.tensor_scalar(half_bits[:], veps[:].bitcast(I32), 1, None, ALU.logical_shift_right))
                last = V_.tensor_scalar(rstd[:].bitcast(I32), half_bits[:], -1.0, float(RSQRT_MAGIC), ALU.mult, ALU.add)
                for _ in range(NEWTON_STEPS):
                    chain(last)
                    chain(V_.tensor_tensor(nt[:], rstd[:], rstd[:], ALU.mult))
                    chain(V_.scalar_tensor_tensor(out=nt[:], in0=nt[:], scalar=-0.5, in1=veps[:], op0=ALU.mult, op1=ALU.mult))
                    last = V_.scalar_tensor_tensor(out=rstd[:], in0=nt[:], scalar=1.5, in1=rstd[:], op0=ALU.add, op1=ALU.mult)
                chain(last)
                for n in range(TILES):
                    last = V_.tensor_scalar(xn[at.stage][:, n, :], xb[:, n, :], mv[:, n, 0:1], rstd[:, n:n + 1],
                                            ALU.subtract, ALU.mult)
                last.then_inc(S["xn_done"], 1)

            def ring(at):
                dve.wait_ge(d_full, at.count("d_full"))
                return dve_ring[at.bank("d_full", D_RING)]

            def xT(at):
                split_done(xT_h[at.stage][:], xT_l[at.stage][:], ring(at)[:]).then_inc(d_done, 1)

            def wide(small):
                return small.unsqueeze(2).to_broadcast([P, TILES, EXPERTS])

            def logits(at):
                bank = ring(at)
                V_.tensor_tensor(lg[:], bank[:, 0:TILES * EXPERTS].rearrange("p (n e) -> p n e", n=TILES),
                                 gate_bias[:], ALU.add).then_inc(d_done, 2)
                dve.wait_ge(d_done, at.count("d_done"))
                chain(V_.tensor_reduce(mx[:], lg[:], AX.X, ALU.max))
                V_.tensor_tensor(lg[:], lg[:], wide(mx[:]), ALU.subtract).then_inc(S["lg_done"], 1)
                dve.wait_ge(S["ex_done"], at.count("ex_done"))
                chain(V_.tensor_reduce(sm[:], ex[:], AX.X, ALU.add))
                chain(V_.reciprocal(rs[:], sm[:]))
                chain(V_.tensor_tensor(pr[:], ex[:], wide(rs[:]), ALU.mult))
                chain(V_.tensor_reduce(m1[:], pr[:], AX.X, ALU.max))
                chain(V_.tensor_tensor(eq[:], pr[:], wide(m1[:]), ALU.is_equal))
                chain(V_.tensor_tensor(cand[:], eq[:], first_wins[:], ALU.mult))
                chain(V_.tensor_reduce(s1[:], cand[:], AX.X, ALU.max))
                chain(V_.tensor_tensor(one1[:], cand[:], wide(s1[:]), ALU.is_equal))
                chain(V_.scalar_tensor_tensor(out=pr2[:], in0=one1[:], scalar=-2.0, in1=pr[:], op0=ALU.mult, op1=ALU.add))
                chain(V_.tensor_reduce(m2[:], pr2[:], AX.X, ALU.max))
                chain(V_.tensor_tensor(eq[:], pr2[:], wide(m2[:]), ALU.is_equal))
                chain(V_.tensor_tensor(cand[:], eq[:], first_wins[:], ALU.mult))
                chain(V_.tensor_reduce(s2[:], cand[:], AX.X, ALU.max))
                chain(V_.tensor_tensor(one2[:], cand[:], wide(s2[:]), ALU.is_equal))
                chain(V_.tensor_tensor(one2[:], one2[:], one1[:], ALU.add))
                V_.scalar_tensor_tensor(out=G[:], in0=pr[:], scalar=0.5, in1=one2[:], op0=ALU.mult,
                                        op1=ALU.mult).then_inc(S["g_done"], 1)

            def gT_(at):
                bank = ring(at)
                rows = gT[at.stage]
                chain(V_.tensor_copy(rows[0:EXPERTS, :], bank[0:EXPERTS, :]))
                V_.tensor_copy(rows[32:32 + EXPERTS, :], rows[0:EXPERTS, :])
                V_.tensor_tensor(rows[64:64 + EXPERTS, :], bank[0:EXPERTS, :], rows[0:EXPERTS, :].bitcast(F32),
                                 ALU.subtract).then_inc(d_done, 1)

            def h(at):
                wait(dve, S["hl_done"], at.count("hl_done", back=H_RING))
                if at.k % 2 == 0:
                    dve.wait_ge(a_done, at.count("a_done", "gb", at.k // 2))
                V_.scalar_tensor_tensor(out=hg[:, at.k % H_RING, :], in0=ring(at)[:], scalar=neg_b1[:, at.k:at.k + 1],
                                        in1=gb[:, (at.k // 2) % GB_RING, :], op0=ALU.max, op1=ALU.mult).then_inc(d_done, 1)

            def back(at):
                xb = X[:, x_place(dve, at), :, :].rearrange("p n d -> p (n d)")
                V_.tensor_tensor(xb, ring(at)[:], xb, ALU.add).then_inc(d_done, 1)

            def qk(at):
                slot, stacked = "qk".index(at.name), at.name + "_stacked"
                wait(dve, S[stacked], at.count(stacked, back=ADDS[stacked][at.name]))
                split_done(nat_h[:, slot, :], nat_l[:, slot, :], ring(at)[:]).then_inc(d_done, 1)

            def max_(at):
                head, n = divmod(at.k, TILES)
                V_.tensor_reduce(neg_m[:, n, head:head + 1], ring(at)[:], AX.X, ALU.max, negate=True).then_inc(d_done, 1)

            def mrow(at):
                bank = ring(at)
                wait(dve, S["m_stacked"], at.count("m_stacked", back=32))
                split_done(mrow_h[:], mrow_l[:], bank[0:GROUP, :]).then_inc(d_done, 1)

            def sum_(at):
                g = at.k
                V_.reciprocal(rden[:], ring(at)[:]).then_inc(d_done, 1)
                dve.wait_ge(d_done, at.count("d_done"))
                V_.tensor_tensor(o_n[:], o_bank[:], rden[:], ALU.mult).then_inc(S["o_read"], 1)
                dve.wait_ge(S["o_read"], at.count("o_read", "sum", g))
                chain(V_.tensor_copy(o_h[:, g, :], o_n[:]))
                V_.tensor_tensor(o_l[:, g, :], o_n[:], o_h[:, g, :].bitcast(F32), ALU.subtract).then_inc(S["o_done"], 1)

            does = {"norm": norm, "xT": xT, "logits": logits, "gT": gT_, "h": h, "back": back, "q": qk, "k": qk,
                    "max": max_, "mrow": mrow, "sum": sum_}
            for step in before:
                if step[2] in does:
                    does[step[2]](At(step, None))
            with dve.Fori(0, LOOPS) as turn:
                linked["turn"], start = turn, linked["n"]
                for step in body:
                    if step[2] in does:
                        does[step[2]](At(step, turn))
                assert linked["n"] - start == per_turn
            linked["n"] += (LOOPS - 1) * per_turn
            linked["turn"] = None
            for step in after:
                if step[2] in does:
                    does[step[2]](At(step, None))

        @block.tensor
        def _(pe):
            def product3(dst, wh, wl, mh, ml, start=True, stop=True):
                pe_mm(dst, wh, mh, start=start, stop=False)
                pe_mm(dst, wl, mh, start=False, stop=False)
                return pe_mm(dst, wh, ml, start=False, stop=stop)

            def pe_mm(dst, w, m, start=True, stop=True):
                return nc.tensor.matmul(dst, w, m, start=start, stop=stop)

            pe.wait_ge(weights_in, 16 * WEIGHT_DMAS)
            pe.wait_ge(consts_made, 1)
            for g in range(GROUPS):
                nc.tensor.transpose(dve_ring[0][:, g * P:(g + 1) * P], wq_raw[:, g, :], ident[:])
                nc.tensor.transpose(dve_ring[0][:, HD + g * D:HD + (g + 1) * D], wo_raw[:, g * P:(g + 1) * P], ident[:])
                nc.tensor.transpose(dve_ring[1][0:RANK, g * P:(g + 1) * P], wk_raw[:, g, :], ident[:])
                nc.tensor.transpose(dve_ring[1][0:RANK, HD + g * P:HD + (g + 1) * P], wv_raw[:, g, :], ident[:])
            nc.tensor.transpose(dve_ring[2][:, 0:EXPERTS], gw_raw, ident[0:EXPERTS, 0:EXPERTS])
            nc.tensor.transpose(dve_ring[2][:, EXPERTS:EXPERTS + UNITS], b1_raw,
                                ident[0:UNITS, 0:UNITS]).then_inc(setup_pe, 1)
            pe.wait_ge(setup_dve, 1)
            pe_mm(act_ring[0][:], down_raw, up_T)
            for u in range(UNITS):
                last = pe_mm(act_ring[1][0:EXPERTS, 0:D], b1_masked[:, u, :], w2_raw[:, u, :],
                             start=(u == 0), stop=(u == UNITS - 1))
            last.then_inc(setup_pe, 1)
            pe.wait_ge(setup_dve, 2)

            def ring_d(at):
                wait(pe, d_done, at.count("d_done", back=D_RING + ADDS["d_full"][at.name] - 1))
                return dve_ring[at.bank("d_full", D_RING)]

            def ring_a(at):
                wait(pe, a_done, at.count("a_done", back=A_RING))
                return act_ring[at.bank("a_full", A_RING)]

            def tokens(n):
                return slice(n * P, (n + 1) * P)

            def xT(at):
                bank = ring_d(at)
                pe.wait_ge(S["xn_done"], at.count("xn_done", "norm", 0))
                for n in range(TILES):
                    last = nc.tensor.transpose(bank[:, tokens(n)], xn[at.stage][:, n, :], ident[:])
                last.then_inc(d_full, 1)

            def logits(at):
                bank = ring_d(at)
                pe.wait_ge(d_done, at.count("d_done", "xT", 0))
                for n in range(TILES):
                    last = product3(bank[:, n * EXPERTS:(n + 1) * EXPERTS], xT_h[at.stage][:, tokens(n)], xT_l[at.stage][:, tokens(n)],
                                    gw_h[:], gw_l[:])
                last.then_inc(d_full, 2)

            def gT_(at):
                bank = ring_d(at)
                pe.wait_ge(S["g_done"], at.count("g_done", "logits", 0))
                for n in range(TILES):
                    last = nc.tensor.transpose(bank[0:EXPERTS, tokens(n)], G[:, n, :], ident[:])
                last.then_inc(d_full, 1)

            def gb_(at):
                bank = ring_a(at)
                if at.k == 0:
                    pe.wait_ge(d_done, at.count("d_done", "gT", 0))
                pe_mm(bank[:], pick[:, at.k, :], gT[at.stage][:]).then_inc(a_full, 1)

            def h(at):
                product3(ring_d(at)[:], w1h[:, at.k * P:(at.k + 1) * P], w1l[:, at.k * P:(at.k + 1) * P],
                         xT_h[at.stage][:], xT_l[at.stage][:]).then_inc(d_full, 1)

            def y(at):
                slot = at.k % H_RING
                pe.wait_ge(S["hl_done"], at.count("hl_done", "h"))
                if at.k == 0:
                    wait(pe, S["yT_done"], at.count("yT_done", "fix", 0, back=1))
                product3(y_bank[:], w2h[:, at.k, :], w2l[:, at.k, :], hh[:, slot, :], hl[:, slot, :],
                         start=at.k == 0, stop=False).then_inc(S["y_used"], 1)

            def fix(at):
                pe_mm(y_bank[:], corr[:], gT[at.stage][:], start=False, stop=True).then_inc(S["y_full"], 1)

            def back(at):
                bank = ring_d(at)
                if at.stage == "B":
                    pe.wait_ge(a_done, at.count("a_done", "wo", 0))
                else:
                    pe.wait_ge(S["yT_done"], at.count("yT_done", "fix", 0))
                for n in range(TILES):
                    last = nc.tensor.transpose(bank[:, tokens(n)], (yT_B if at.stage == "B" else yT)[:, tokens(n)], ident[:])
                last.then_inc(d_full, 1)

            def qk(at):
                bank, kind, g = ring_d(at), "qk".index(at.name), at.k
                if at.k == 0:
                    pe.wait_ge(d_done, at.count("d_done", "xT", 0))
                product3(bank[:], wqkv_h[:, kind, g * P:(g + 1) * P], wqkv_l[:, kind, g * P:(g + 1) * P],
                         xT_h[at.stage][:], xT_l[at.stage][:]).then_inc(d_full, 1)

            def v(at):
                bank = ring_a(at)
                for i in range(2):
                    n = 2 * at.k + i
                    last = product3(bank[:, i * HD:(i + 1) * HD], xT_h[at.stage][:, tokens(n)], xT_l[at.stage][:, tokens(n)],
                                    wqkv_h[:, 2, :], wqkv_l[:, 2, :])
                last.then_inc(a_full, 1)

            def max_(at):
                head, n = divmod(at.k, TILES)
                bank = ring_d(at)
                if at.k % (GROUP * TILES) == 0:
                    pe.wait_ge(S["q_stacked"], at.count("q_stacked", "q", head // GROUP))
                    pe.wait_ge(S["k_stacked"], at.count("k_stacked", "k", head // GROUP))
                pe_mm(bank[:], qs[0:STACK, head, tokens(n)], ks[0:STACK, head, :]).then_inc(d_full, 1)

            def mrow(at):
                bank = ring_d(at)
                pe.wait_ge(d_done, at.count("d_done", "max", (at.k + 1) * GROUP * TILES - 1))
                for n in range(TILES):
                    last = nc.tensor.transpose(bank[0:GROUP, tokens(n)], neg_m[:, n, at.k * GROUP:(at.k + 1) * GROUP],
                                               ident[:])
                last.then_inc(d_full, 1)

            def s_(at):
                m, j = divmod(at.k, GROUP)
                g, kt = divmod(m, TILES)
                bank = ring_a(at)
                if kt == 0 and j == 0:
                    pe.wait_ge(S["m_stacked"], at.count("m_stacked", "mrow", g))
                head = g * GROUP + j
                pe_mm(bank[:], ks[:, head, tokens(kt)], qs[:, head, :]).then_inc(a_full, 1)

            def pv(at):
                g, kt = divmod(at.k, TILES)
                pe.wait_ge(a_done, at.count("a_done", "s", at.k * GROUP + GROUP - 1))
                if kt == 0:
                    wait(pe, S["o_read"], at.count("o_read", "sum", g, back=1))
                for j in range(GROUP):
                    head = g * GROUP + j
                    last = nc.tensor.matmul(o_bank[j * DH:(j + 1) * DH, :], V[:, kt, head * DH:(head + 1) * DH],
                                            probs[:, at.k % P_RING, j, :], start=kt == 0, stop=kt == TILES - 1)
                last.then_inc(S["p_used"], 1)

            def sum_(at):
                bank = ring_d(at)
                pe.wait_ge(S["p_added"], at.count("p_added", "add", (at.k + 1) * TILES * GROUP - 1))
                for j in range(GROUP):
                    last = nc.tensor.matmul(bank[j * DH:(j + 1) * DH, :], ones[:], probs[:, TILES - 1, j, :], start=True, stop=True)
                last.then_inc(d_full, 1)

            def wo_(at):
                bank = ring_a(at)
                pe.wait_ge(S["o_done"], at.count("o_done", "sum", GROUPS - 1))
                for g in range(GROUPS):
                    last = product3(bank[:], wo_h[:, g, :], wo_l[:, g, :], o_h[:, g, :], o_l[:, g, :],
                                    start=g == 0, stop=g == GROUPS - 1)
                last.then_inc(a_full, 1)

            walk(pe, {"xT": xT, "logits": logits, "gT": gT_, "gb": gb_, "h": h, "y": y, "fix": fix, "back": back,
                      "q": qk, "k": qk, "v": v, "max": max_, "mrow": mrow, "s": s_, "pv": pv, "sum": sum_, "wo": wo_})


_INS = ['L0_attn_x', 'L0_attn_Wq', 'L0_attn_Wkv_down', 'L0_attn_Wk_up', 'L0_attn_Wv_up', 'L0_attn_Wo',
        'L0_ffn_gate_w', 'L0_ffn_gate_b', 'L0_ffn_w1', 'L0_ffn_b1', 'L0_ffn_w2', 'L0_ffn_b2']


def kernel(**inputs):
    import numpy as _np
    import concourse.bacc as _bacc
    from concourse import mybir as _mybir
    from concourse.bass_utils import run_bass_kernel_spmd as _run

    nc = _bacc.Bacc("TRN2", target_bir_lowering=False, num_devices=1)
    arrays, args = {}, []
    for name in _INS:
        a = _np.ascontiguousarray(inputs[name])
        arrays[f"in_{name}_dram"] = a
        args.append(nc.dram_tensor(f"in_{name}_dram", a.shape, _mybir.dt.from_np(a.dtype), kind="ExternalInput").ap())
    shape = inputs['L0_attn_x'].shape
    args.append(nc.dram_tensor("out_0_dram", shape, _mybir.dt.float32, kind="ExternalOutput").ap())
    macaron_kernel(nc, *args)
    r = _run(nc, [arrays], core_ids=[0])
    return r.results[0]["out_0_dram"]
```

```python
from contextlib import ExitStack

import concourse.bass as bass
from concourse import mybir
from concourse.alu_op_type import AluOpType as ALU

F32 = mybir.dt.float32
F32R = mybir.dt.float32r
ACT = mybir.ActivationFunctionType
AX = mybir.AxisListType

P = 128
EPS = 1e-5

EXPERTS, UNITS = 8, 16
TILES, HEADS, GROUP = 4, 8, 4
GROUPS = HEADS // GROUP
START = {"A": 0, "B": 2 * UNITS + 0.21, "C": 5 * UNITS + 0.0}
LOAD = -11.97
Y_LAG = 4.12
FFN = {
    "A": {"norm": -8.17, "scaled": -7.17, "xT": -5.85, "logits": -3.99, "top1": -3.41, "top2": -2.62,
          "gT": -1.81, "gb": -1.26, "gb_ahead": -0.11, "fix": 19.22, "back": 21.56},
    "C": {"norm": -8.06, "scaled": -6.51, "xT": -5.87, "logits": -5.0, "top1": -4.37, "top2": -3.24,
          "gT": -1.34, "gb": -0.49, "gb_ahead": 1.39, "fix": 19.22, "back": 21.93},
}
PREPARE = {"norm": -9.83, "scaled": -9.32, "xT": -7.88}
PROJECT = {("q", 0): -7.17, ("k", 0): -5.99, ("v", 0): 2.05, ("v", 1): 5.18, ("q", 1): 4.3, ("k", 1): 4.94}
GROUP_SLOTS = (
    {"max": 0.0, "max_pace": 0.62, "mrow": 0.81, "s": 1.43, "s_pace": 0.617, "pv_first": 1.95,
     "pv": 0.82, "add_pace": 0.683, "sum": 2.28, "onorm": 1.33, "oh": 1.45},
    {"max": 10.91, "max_pace": 0.62, "mrow": -0.04, "s": 1.4, "s_pace": 0.612, "pv_first": 1.35,
     "pv": 0.69, "add_pace": 0.555, "sum": 2.42, "onorm": 0.99, "oh": 1.56},
)
WO, B_BACK = 2.38, 3.5


def batch_steps():
    steps = [(LOAD, "A", "load", 0)]
    for stage in "AC":
        c, start = FFN[stage], START[stage]
        for name in ("norm", "scaled", "xT", "logits", "top1", "top2", "gT", "gb"):
            steps.append((start + c[name], stage, name, 0))
        for u in range(UNITS):
            if u % 2 and u + 1 < UNITS:
                steps.append((start + u - c["gb_ahead"], stage, "gb", (u + 1) // 2))
            steps.append((start + u, stage, "h", u))
            steps.append((start + u + Y_LAG, stage, "y", u))
        steps.append((start + c["fix"], stage, "fix", 0))
        steps.append((start + c["back"], stage, "back", 0))
    steps.append((START["C"] + FFN["C"]["back"] + 0.3, "C", "store", 0))
    b = START["B"]
    steps += [(b + slot, "B", name, 0) for name, slot in PREPARE.items()]
    steps += [(b + slot, "B", name, k) for (name, k), slot in PROJECT.items()]
    for g, c in enumerate(GROUP_SLOTS):
        for n in range(GROUP * TILES):
            steps.append((b + c["max"] + n * c["max_pace"], "B", "max", g * GROUP * TILES + n))
        end = b + c["max"] + GROUP * TILES * c["max_pace"]
        steps.append((end + c["mrow"], "B", "mrow", g))
        for n in range(GROUP * TILES):
            steps.append((end + c["s"] + n * c["s_pace"], "B", "s", g * GROUP * TILES + n))
        for kt in range(TILES):
            pv = end + c["s"] + (kt + 1) * GROUP * c["s_pace"] + c["pv" if kt else "pv_first"]
            steps.append((pv, "B", "pv", g * TILES + kt))
            for j in range(GROUP if kt else 0):
                steps.append((pv + (j + 1) * c["add_pace"], "B", "add", (g * TILES + kt) * GROUP + j))
        done = pv + c["sum"]
        steps += [(done, "B", "sum", g), (done + c["onorm"], "B", "onorm", g), (done + c["oh"], "B", "oh", g)]
    steps += [(done + WO, "B", "wo", 0), (done + B_BACK, "B", "back", 0)]
    return steps


def turn_steps(t, batches):
    found = []
    for order, (slot, stage, name, k) in enumerate(batch_steps()):
        later, place = divmod(slot, 2 * UNITS)
        if 0 <= t - int(later) < batches:
            found.append((place, order, (stage, t - int(later), name, k)))
    return [step for _, _, step in sorted(found)]


ADDS = {
    "d_full": {"xT": 1, "logits": 2, "gT": 1, "h": 1, "back": 1, "q": 1, "k": 1, "max": 1, "mrow": 2},
    "a_full": {"v": 1, "s": 1, "wo": 2, "sum": 1},
    "mv_done": {"norm": 1},
    "rstd_done": {"norm": 1},
    "xn_done": {"scaled": 1},
    "lg_done": {"logits": 1},
    "ex_done": {"logits": 1},
    "g_done": {"top2": 1},
    "hi_done": {"xT": 1, "gT": 1, "mrow": 1, "q": 1, "k": 1},
    "g_saved": {"gT": 16},
    "gb_in": {"gb": 16},
    "y_used": {"y": 1},
    "y_full": {"fix": 1},
    "yT_done": {"fix": 1},
    "q_stacked": {"q": 16 * 3 * GROUP},
    "k_stacked": {"k": 16 * 3 * GROUP},
    "m_stacked": {"mrow": 32},
    "p_used": {"pv": 1},
    "p_added": {"add": 1},
    "o_read": {"onorm": 1},
    "oh_done": {"oh": 1},
    "o_done": {"oh": 1},
    "x_in": {"load": 16},
    "x_out": {"store": 16},
}
ADDS["d_done"] = ADDS["d_full"]
ADDS["a_done"] = ADDS["a_full"]


def macaron_kernel(nc, x, wq, wkv_down, wk_up, wv_up, wo, gate_w, gate_b, w1, b1, w2, b2, out):
    BATCHES, TOKENS, D = x.shape
    HID = w1.shape[2]
    RANK = wkv_down.shape[0]
    HD = wq.shape[0]
    DH = HD // HEADS
    SCALE = float(DH) ** -0.5
    assert D == P and TOKENS == TILES * P and HID == 2 * P and HD == GROUPS * P and w1.shape[0] == EXPERTS
    STACK = 3 * DH
    KROWS = STACK + 2
    GROWS = 72
    D_RING, A_RING, X_RING = 4, 2, 4
    H_RING, GB_RING, P_RING = 8, 4, TILES

    FIRST_LOOPED, BODY_TURNS = 3, X_RING
    LOOPS = (BATCHES - 1 - FIRST_LOOPED) // BODY_TURNS
    FIRST_AFTER = FIRST_LOOPED + LOOPS * BODY_TURNS
    turns = {t: turn_steps(t, BATCHES) for t in range(-1, BATCHES + 3)}
    before = [st for t in range(-1, FIRST_LOOPED) for st in turns[t]]
    body = [st for t in range(FIRST_LOOPED, FIRST_LOOPED + BODY_TURNS) for st in turns[t]]
    after = [st for t in range(FIRST_AFTER, BATCHES + 3) for st in turns[t]]
    per_body = {sem: sum(adds.get(st[2], 0) for st in body) for sem, adds in ADDS.items()}
    assert per_body["d_full"] % D_RING == 0 and per_body["a_full"] % A_RING == 0
    counts = {}
    for sem, adds in ADDS.items():
        n = 0
        for st in before + [st for t in range(FIRST_LOOPED, BATCHES + 3) for st in turns[t]]:
            n += adds.get(st[2], 0)
            if st[2] in adds:
                counts[sem, st] = n

    with ExitStack() as ctx:
        def sb(name, shape, dt=F32):
            return ctx.enter_context(nc.sbuf_tensor(name, shape, dt))

        def sem(name):
            return ctx.enter_context(nc.semaphore(name))

        X = sb("X", [P, X_RING, TILES, D])
        w1h, w1l = sb("w1h", [P, EXPERTS * HID], F32R), sb("w1l", [P, EXPERTS * HID], F32R)
        w2_sb = sb("w2_sb", [P, UNITS, D])
        wqkv_h, wqkv_l = sb("wqkv_h", [P, 3, HD], F32R), sb("wqkv_l", [P, 3, HD], F32R)
        wo_h, wo_l = sb("wo_h", [P, GROUPS, D], F32R), sb("wo_l", [P, GROUPS, D], F32R)
        gw_h, gw_l = sb("gw_h", [P, EXPERTS], F32R), sb("gw_l", [P, EXPERTS], F32R)
        neg_b1 = sb("neg_b1", [P, UNITS])
        b1_masked = sb("b1_masked", [P, UNITS, EXPERTS])
        gate_bias = sb("gate_bias", [P, TILES, EXPERTS])
        first_wins = sb("first_wins", [P, TILES, EXPERTS])
        b2_sb = sb("b2_sb", [EXPERTS, D])
        corr_f = sb("corr_f", [EXPERTS, D])
        corr = sb("corr", [GROWS, D], F32R)
        ident = sb("ident", [P, P])
        ones = sb("ones", [P, DH])
        stats, mv = sb("stats", [P, TILES, 6]), sb("mv", [P, TILES, 2])
        veps, rstd, nt = sb("veps", [P, TILES]), sb("rstd", [P, TILES]), sb("nt", [P, TILES])
        aggr_wait = sb("aggr_wait", [P, 1])
        xn = {s: sb("xn" + s, [P, TILES, D]) for s in "ABC"}
        xT_h = {s: sb("xT_h" + s, [P, TOKENS], F32R) for s in "ABC"}
        xT_l = {s: sb("xT_l" + s, [P, TOKENS], F32R) for s in "ABC"}
        lg, ex, pr = (sb(n, [P, TILES, EXPERTS]) for n in ("lg", "ex", "pr"))
        eq, cand, one1, one2, pr2, G = (sb(n, [P, TILES, EXPERTS]) for n in ("eq", "cand", "one1", "one2", "pr2", "G"))
        mx, sm, rs, m1, s1, m2, s2 = (sb(n, [P, TILES]) for n in ("mx", "sm", "rs", "m1", "s1", "m2", "s2"))
        gT = {s: sb("gT" + s, [GROWS, TOKENS], F32R) for s in "AC"}
        gT_f = sb("gT_f", [EXPERTS, TOKENS])
        gb = sb("gb", [P, GB_RING, TOKENS])
        hg = sb("hg", [P, H_RING, TOKENS])
        yT, yT_B = sb("yT", [P, TOKENS]), sb("yT_B", [P, TOKENS])
        nat_h, nat_l = sb("nat_h", [P, 2, TOKENS], F32R), sb("nat_l", [P, 2, TOKENS], F32R)
        qs, ks = sb("qs", [KROWS, HEADS, TOKENS], F32R), sb("ks", [KROWS, HEADS, TOKENS], F32R)
        V = sb("V", [P, TILES, HD])
        neg_m = sb("neg_m", [P, TILES, HEADS])
        mrow_h, mrow_l = sb("mrow_h", [GROUP, TOKENS], F32R), sb("mrow_l", [GROUP, TOKENS], F32R)
        probs = sb("probs", [P, P_RING, GROUP, TOKENS])
        rden, o_n = sb("rden", [P, TOKENS]), sb("o_n", [P, TOKENS])
        o_h, o_l = sb("o_h", [P, GROUPS, TOKENS], F32R), sb("o_l", [P, GROUPS, TOKENS], F32R)
        up_T = hg[0:RANK, 2, :]
        w1_raw = probs[:, 0, :, :].rearrange("p a n -> p (a n)")
        wq_raw = probs[:, 2, 0, 0:GROUPS * D].rearrange("p (g d) -> p g d", g=GROUPS)
        wo_raw = probs[:, 2, 0, 256:256 + HD]
        wk_raw = probs[:, 2, 1, 0:GROUPS * RANK].rearrange("p (g r) -> p g r", g=GROUPS)
        wv_raw = probs[:, 2, 1, 128:128 + GROUPS * RANK].rearrange("p (g r) -> p g r", g=GROUPS)
        down_raw = probs[0:RANK, 2, 1, 256:256 + D]
        gw_raw = probs[0:EXPERTS, 2, 2, 0:D]
        b1_raw = probs[0:UNITS, 2, 2, 128:128 + P]

        dve_ring = [ctx.enter_context(nc.psum_tensor(f"dve_ring{i}", [P, TOKENS], F32)) for i in range(D_RING)]
        act_ring = [ctx.enter_context(nc.psum_tensor(f"act_ring{i}", [P, TOKENS], F32)) for i in range(A_RING)]
        y_bank = ctx.enter_context(nc.psum_tensor("y_bank", [P, TOKENS], F32))
        o_bank = ctx.enter_context(nc.psum_tensor("o_bank", [P, TOKENS], F32))

        S = {name: sem(name) for name in ADDS}
        gb_in = [sem(f"gb_in{i}") for i in range(GB_RING)]
        d_full, d_done, a_full, a_done = S["d_full"], S["d_done"], S["a_full"], S["a_done"]
        weights_in = sem("weights_in")
        consts_made = sem("consts_made")
        setup_pe = sem("setup_pe")
        setup_dve = sem("setup_dve")
        link = sem("link")
        pool_link = sem("pool_link")
        act_link = sem("act_link")

        class At:

            def __init__(self, step, turn):
                self.stage, _, self.name, self.k = self.step = step
                self.turn = turn
                self.batch = step[1] if turn is None else turn * BODY_TURNS + step[1]

            def count(self, name, step=None, k=None, back=0, batch=0, stage=None):
                def key(turn):
                    return (name, (stage or self.stage, self.step[1] + batch + turn * BODY_TURNS, step or self.name,
                                   self.k if k is None else k))
                if self.turn is None:
                    return counts.get(key(0), 0) - back
                n = counts[key(0)] - back
                assert all(counts[key(i)] - back == n + i * per_body[name] for i in range(LOOPS)), (name, self.step)
                return n + self.turn * per_body[name]

            def gb_count(self, k):
                i = counts["gb_in", (self.stage, self.step[1], "gb", k)] // 16 - 1
                n = 16 * (i // GB_RING + 1)
                assert i % GB_RING == k % GB_RING and per_body["gb_in"] % GB_RING == 0
                return n if self.turn is None else n + self.turn * (per_body["gb_in"] // GB_RING)

            def bank(self, name, ring):
                return (counts[name, self.step] - ADDS[name][self.name]) % ring

        def x_place(at):
            return at.step[1] % X_RING

        def wait(eng, semaphore, value):
            if isinstance(value, int) and value <= 0:
                return
            eng.wait_ge(semaphore, value)

        class Chain:

            def __init__(self, eng, semaphore, per_step):
                self.eng, self.semaphore, self.n, self.turn = eng, semaphore, 0, None
                self.per_turn = sum(per_step.get(st[2], 0) for st in body)

            def __call__(self, ins):
                self.n += 1
                ins.then_inc(self.semaphore, 1)
                self.eng.wait_ge(self.semaphore, self.n if self.turn is None else self.n + self.turn * self.per_turn)

        def walk(eng, does, chain=None, setup={}):
            for n, step in enumerate(before):
                if n < len(turns[-1]) and step[2] in setup:
                    setup[step[2]]()
                if step[2] in does:
                    does[step[2]](At(step, None))
            start = chain.n if chain else 0
            with eng.Fori(0, LOOPS) as turn:
                if chain:
                    chain.turn = turn
                for step in body:
                    if step[2] in does:
                        does[step[2]](At(step, turn))
            if chain:
                assert chain.n - start == chain.per_turn
                chain.n += (LOOPS - 1) * chain.per_turn
                chain.turn = None
            for step in after:
                if step[2] in does:
                    does[step[2]](At(step, None))

        gates = {s: nc.dram_tensor("gates_" + s, (EXPERTS, TOKENS), F32).ap() for s in "AC"}

        WEIGHT_DMAS = 10 + TILES

        block = ctx.enter_context(nc.Block())

        @block.sync
        def _(sp):
            x_v = x.rearrange("b (p n) d -> b p n d", n=TILES)
            out_v = out.rearrange("b (p n) d -> b p n d", n=TILES)

            def load(at):
                place = x_place(at)
                if at.turn is None:
                    wait(sp, S["xn_done"], at.count("xn_done", "scaled", batch=-1))
                wait(sp, S["x_out"], at.count("x_out", "store", stage="C", batch=-X_RING))
                sp.dma_start(X[:, place, :, :], x_v[at.batch]).then_inc(S["x_in"], 16)

            def qk(at):
                sp.wait_ge(d_done, at.count("d_done"))
                kind, g = "qk".index(at.name), at.k
                stack = (qs, ks)[kind]
                halves = ((nat_h, nat_h, nat_l), (nat_h, nat_l, nat_h))[kind]
                for j in range(GROUP):
                    for r, half in enumerate(halves):
                        sp.dma_start(stack[r * DH:(r + 1) * DH, g * GROUP + j, :].bitcast(F32),
                                     half[j * DH:(j + 1) * DH, kind, :].bitcast(F32)).then_inc(S[at.name + "_stacked"], 16)

            def mrow(at):
                sp.wait_ge(d_done, at.count("d_done"))
                for r, row in enumerate((mrow_h, mrow_l)):
                    sp.dma_start(qs[STACK + r:STACK + r + 1, at.k * GROUP:(at.k + 1) * GROUP, :].rearrange("p h n -> p (h n)")
                                 .bitcast(F32), row[:].bitcast(F32)).then_inc(S["m_stacked"], 16)

            def store(at):
                place = x_place(at)
                sp.wait_ge(d_done, at.count("d_done", "back", 0))
                sp.dma_start(out_v[at.batch], X[:, place, :, :]).then_inc(S["x_out"], 16)

            walk(sp, {"load": load, "q": qk, "k": qk, "mrow": mrow, "store": store})
            sp.wait_ge(S["x_out"], 16 * BATCHES)

        @block.gpsimd
        def _(pool):
            pool.memset(ident[:], 0.0).then_inc(pool_link, 1)
            pool.memset(ones[:], 1.0)
            for e in range(EXPERTS):
                pool.memset(first_wins[:, :, e:e + 1], float(EXPERTS - e))
            pool.wait_ge(pool_link, 1)
            pool.affine_select(out=ident[:], in_=ident[:], compare_op=ALU.not_equal, fill=1.0, base=0,
                               pattern=[[-1, P]], channel_multiplier=1).then_inc(consts_made, 1)

            def oh(at):
                pool.wait_ge(S["oh_done"], at.count("oh_done"))
                pool.tensor_tensor(o_l[:, at.k, :], o_n[:], o_h[:, at.k, :].bitcast(F32),
                                 ALU.subtract).then_inc(S["o_done"], 1)

            def add(at):
                m, j = divmod(at.k, GROUP)
                kt = m % TILES
                pool.wait_ge(S["p_used"], at.count("p_used", "pv", m))
                if kt > 1:
                    pool.wait_ge(S["p_added"], at.count("p_added", "add", at.k - GROUP))
                pool.tensor_tensor(probs[:, kt, j, :], probs[:, kt - 1, j, :], probs[:, kt, j, :],
                                   ALU.add).then_inc(S["p_added"], 1)

            walk(pool, {"oh": oh, "add": add})

        @block.scalar
        def _(act):
            for dst, src in (
                (wq_raw, wq.rearrange("(g p) d -> p g d", p=P)), (wo_raw, wo),
                (wk_raw, wk_up.rearrange("(g p) r -> p g r", p=P)),
                (wv_raw, wv_up.rearrange("(g p) r -> p g r", p=P)),
                (down_raw, wkv_down), (gw_raw, gate_w),
                (b1_raw, b1.rearrange("e (h p) -> (e h) p", p=P)),
                (w2_sb[:], w2.rearrange("e (h p) d -> p (e h) d", p=P)),
                (w1_raw.rearrange("p (e h) -> p e h", e=EXPERTS), w1.rearrange("e p h -> p e h")),
                (b2_sb[:], b2),
            ) + tuple((gate_bias[:, n, :], gate_b.partition_broadcast(P)) for n in range(TILES)):
                act.dma_start(dst, src).then_inc(weights_in, 16)

            act.preload_act_table_set("natural_log_exp_and_others")

            chain = Chain(act, act_link, {"norm": 1, "sum": 1})

            def norm(at):
                act.wait_ge(S["mv_done"], at.count("mv_done"))
                chain(act.activation(rstd[:], veps[:], ACT.Ln))
                act.activation(rstd[:], rstd[:], ACT.Exp, scale=-0.5).then_inc(S["rstd_done"], 1)

            def logits(at):
                act.wait_ge(S["lg_done"], at.count("lg_done"))
                act.activation(ex[:], lg[:], ACT.Exp).then_inc(S["ex_done"], 1)

            def gated(at):
                return at.count("y_used", "y", 2 * at.k + 1, back=2 * GB_RING)

            def gb_(at):
                if at.k == 0:
                    act.wait_ge(S["g_saved"], at.count("g_saved", "gT"))
                wait(act, S["y_used"], gated(at))
                act.dma_start(gb[:, at.k % GB_RING, :], gates[at.stage][at.k].partition_broadcast(P)).then_inc(
                    gb_in[at.k % GB_RING], 16)

            def fix(at):
                act.wait_ge(S["y_full"], at.count("y_full"))
                act.activation(yT[:], y_bank[:], ACT.Copy).then_inc(S["yT_done"], 1)

            def v(at):
                act.wait_ge(a_full, at.count("a_full"))
                act.activation(V[:, 2 * at.k:2 * at.k + 2, :].rearrange("p n d -> p (n d)"),
                               act_ring[at.bank("a_full", A_RING)][:], ACT.Copy).then_inc(a_done, 1)

            def s_(at):
                m, j = divmod(at.k, GROUP)
                g, kt = divmod(m, TILES)
                act.wait_ge(a_full, at.count("a_full"))
                if j == 0:
                    last_group = {"k": GROUPS - 1, "batch": -1} if g == 0 else {"k": g - 1}
                    if kt < TILES - 1:
                        last_group["k"] = (last_group["k"] * TILES + kt + 2) * GROUP - 1
                        wait(act, S["p_added"], at.count("p_added", "add", **last_group))
                    else:
                        wait(act, a_full, at.count("a_full", "sum", **last_group))
                act.activation(probs[:, m % P_RING, j, :], act_ring[at.bank("a_full", A_RING)][:],
                               ACT.Exp, scale=SCALE).then_inc(a_done, 1)

            def wo_(at):
                act.wait_ge(a_full, at.count("a_full"))
                act.activation(yT_B[:], act_ring[at.bank("a_full", A_RING)][:], ACT.Copy).then_inc(a_done, 2)

            def high(at, hi):
                act.wait_ge(d_full, at.count("d_full"))
                act.activation(hi, dve_ring[at.bank("d_full", D_RING)][0:hi.shape[0], :], ACT.Copy).then_inc(S["hi_done"], 1)

            def xT(at):
                high(at, xT_h[at.stage][:])

            def qk(at):
                slot, stacked = "qk".index(at.name), at.name + "_stacked"
                wait(act, S[stacked], at.count(stacked, back=ADDS[stacked][at.name]))
                high(at, nat_h[:, slot, :])

            def gT_(at):
                act.wait_ge(d_full, at.count("d_full"))
                wait(act, S["g_saved"], at.count("g_saved", back=16))
                act.activation(gT_f[:], dve_ring[at.bank("d_full", D_RING)][0:EXPERTS, :], ACT.Copy)
                act.activation(gT[at.stage][32:32 + EXPERTS, :], dve_ring[at.bank("d_full", D_RING)][0:EXPERTS, :], ACT.Copy)
                high(at, gT[at.stage][0:EXPERTS, :])
                act.wait_ge(S["hi_done"], at.count("hi_done"))
                act.dma_start(gates[at.stage], gT_f[:]).then_inc(S["g_saved"], 16)

            def mrow(at):
                wait(act, S["m_stacked"], at.count("m_stacked", back=32))
                high(at, mrow_h[:])

            def sum_(at):
                act.wait_ge(a_full, at.count("a_full"))
                wait(act, S["o_done"], at.count("o_done", "oh", back=1))
                bank = act_ring[at.bank("a_full", A_RING)]
                act.activation(o_n[:], bank[:], ACT.Copy)
                chain(act.activation(rden[:], bank[:], ACT.Ln))
                act.activation(rden[:], rden[:], ACT.Exp, scale=-1.0).then_inc(a_done, 1)

            def oh(at):
                act.wait_ge(S["o_read"], at.count("o_read", "onorm"))
                act.activation(o_h[:, at.k, :], o_n[:], ACT.Copy).then_inc(S["oh_done"], 1)

            walk(act, {"logits": logits, "gb": gb_, "fix": fix, "v": v, "s": s_, "sum": sum_,
                       "oh": oh, "wo": wo_, "norm": norm, "xT": xT, "gT": gT_, "mrow": mrow,
                       "q": qk, "k": qk}, chain)

        @block.vector
        def _(dve):
            V_ = nc.vector
            chain = Chain(dve, link, {"norm": 2, "scaled": 3, "logits": 1, "top1": 8, "top2": 7, "onorm": 2})

            def split_done(hi, lo, src):
                chain(V_.tensor_copy(hi, src))
                return V_.tensor_tensor(lo, src, hi.bitcast(F32), ALU.subtract)

            V_.memset(corr[:].bitcast(F32), 0.0)
            for s in "AC":
                V_.memset(gT[s][:].bitcast(F32), 0.0)
            V_.memset(b1_masked[:], 0.0)
            V_.memset(ks[STACK:KROWS, :, :].bitcast(F32), 1.0)

            def split_weights():
                dve.wait_ge(setup_pe, 1)
                split_done(gw_h[:], gw_l[:], y_bank[:, 0:EXPERTS])
                V_.tensor_copy(up_T, act_ring[1][0:RANK, :])
                for e in range(EXPERTS):
                    V_.tensor_copy(b1_masked[:, 2 * e:2 * e + 2, e], y_bank[:, EXPERTS + 2 * e:EXPERTS + 2 * e + 2])
                V_.tensor_scalar(neg_b1[:], y_bank[:, EXPERTS:EXPERTS + UNITS], -1.0, None,
                                 ALU.mult).then_inc(setup_dve, 1)

            def split_more():
                split_done(w1h[:], w1l[:], w1_raw)
                split_done(wqkv_h[:, 0, :], wqkv_l[:, 0, :], o_bank[:, 0:HD])
                split_done(wo_h[:].rearrange("p g d -> p (g d)"), wo_l[:].rearrange("p g d -> p (g d)"),
                           o_bank[:, HD:HD + GROUPS * D])
                dve.wait_ge(setup_pe, 2)
                split_done(wqkv_h[:, 1:3, :].rearrange("p a n -> p (a n)"),
                           wqkv_l[:, 1:3, :].rearrange("p a n -> p (a n)"), act_ring[0][:])
                chain(V_.tensor_tensor(corr_f[:], act_ring[1][0:EXPERTS, 0:D], b2_sb[:], ALU.add))
                chain(V_.tensor_copy(corr[0:EXPERTS, :], corr_f[:]))
                V_.tensor_copy(corr[64:64 + EXPERTS, :], corr[0:EXPERTS, :])
                V_.tensor_tensor(corr[32:32 + EXPERTS, :], corr_f[:], corr[0:EXPERTS, :].bitcast(F32),
                                 ALU.subtract).then_inc(setup_dve, 1)

            def norm(at):
                xb = X[:, x_place(at), :, :]
                if at.stage == "A":
                    dve.wait_ge(S["x_in"], at.batch * 16 + 16)
                else:
                    dve.wait_ge(d_done, at.count("d_done", "back", stage="AB"["BC".index(at.stage)]))
                V_.memset(aggr_wait[:], 0.0)
                for n in range(TILES):
                    last = V_.bn_stats(out=stats[:, n, :], in_=xb[:, n, :])
                chain(last)
                V_.memset(aggr_wait[:], 0.0)
                for n in range(TILES):
                    last = V_.bn_aggr(mv[:, n, :], stats[:, n, :])
                chain(last)
                V_.tensor_scalar(veps[:], mv[:, :, 1], EPS, None, ALU.add).then_inc(S["mv_done"], 1)

            def scaled(at):
                xb = X[:, x_place(at), :, :]
                dve.wait_ge(S["rstd_done"], at.count("rstd_done", "norm"))
                chain(V_.tensor_tensor(nt[:], rstd[:], rstd[:], ALU.mult))
                chain(V_.scalar_tensor_tensor(out=nt[:], in0=nt[:], scalar=-0.5, in1=veps[:], op0=ALU.mult, op1=ALU.mult))
                chain(V_.scalar_tensor_tensor(out=rstd[:], in0=nt[:], scalar=1.5, in1=rstd[:], op0=ALU.add, op1=ALU.mult))
                for n in range(TILES):
                    last = V_.tensor_scalar(xn[at.stage][:, n, :], xb[:, n, :], mv[:, n, 0:1], rstd[:, n:n + 1],
                                            ALU.subtract, ALU.mult)
                last.then_inc(S["xn_done"], 1)

            def ring(at):
                dve.wait_ge(d_full, at.count("d_full"))
                return dve_ring[at.bank("d_full", D_RING)]

            def low(at, lo, hi):
                dve.wait_ge(S["hi_done"], at.count("hi_done"))
                V_.tensor_tensor(lo, dve_ring[at.bank("d_full", D_RING)][0:hi.shape[0], :], hi.bitcast(F32),
                                 ALU.subtract).then_inc(d_done, ADDS["d_done"][at.name])

            def xT(at):
                low(at, xT_l[at.stage][:], xT_h[at.stage][:])

            def wide(small):
                return small.unsqueeze(2).to_broadcast([P, TILES, EXPERTS])

            def logits(at):
                bank = ring(at)
                V_.tensor_tensor(lg[:], bank[:, 0:TILES * EXPERTS].rearrange("p (n e) -> p n e", n=TILES),
                                 gate_bias[:], ALU.add).then_inc(d_done, 2)
                dve.wait_ge(d_done, at.count("d_done"))
                chain(V_.tensor_reduce(mx[:], lg[:], AX.X, ALU.max))
                V_.tensor_tensor(lg[:], lg[:], wide(mx[:]), ALU.subtract).then_inc(S["lg_done"], 1)

            def top1(at):
                dve.wait_ge(S["ex_done"], at.count("ex_done", "logits"))
                chain(V_.tensor_reduce(sm[:], ex[:], AX.X, ALU.add))
                chain(V_.reciprocal(rs[:], sm[:]))
                chain(V_.tensor_tensor(pr[:], ex[:], wide(rs[:]), ALU.mult))
                chain(V_.tensor_reduce(m1[:], pr[:], AX.X, ALU.max))
                chain(V_.tensor_tensor(eq[:], pr[:], wide(m1[:]), ALU.is_equal))
                chain(V_.tensor_tensor(cand[:], eq[:], first_wins[:], ALU.mult))
                chain(V_.tensor_reduce(s1[:], cand[:], AX.X, ALU.max))
                chain(V_.tensor_tensor(one1[:], cand[:], wide(s1[:]), ALU.is_equal))

            def top2(at):
                chain(V_.scalar_tensor_tensor(out=pr2[:], in0=one1[:], scalar=-2.0, in1=pr[:], op0=ALU.mult, op1=ALU.add))
                chain(V_.tensor_reduce(m2[:], pr2[:], AX.X, ALU.max))
                chain(V_.tensor_tensor(eq[:], pr2[:], wide(m2[:]), ALU.is_equal))
                chain(V_.tensor_tensor(cand[:], eq[:], first_wins[:], ALU.mult))
                chain(V_.tensor_reduce(s2[:], cand[:], AX.X, ALU.max))
                chain(V_.tensor_tensor(one2[:], cand[:], wide(s2[:]), ALU.is_equal))
                chain(V_.tensor_tensor(one2[:], one2[:], one1[:], ALU.add))
                V_.scalar_tensor_tensor(out=G[:], in0=pr[:], scalar=0.5, in1=one2[:], op0=ALU.mult,
                                        op1=ALU.mult).then_inc(S["g_done"], 1)

            def gT_(at):
                low(at, gT[at.stage][64:64 + EXPERTS, :], gT[at.stage][0:EXPERTS, :])

            def h(at):
                wait(dve, S["y_used"], at.count("y_used", "y", back=H_RING))
                if at.k % 2 == 0:
                    dve.wait_ge(gb_in[at.k // 2 % GB_RING], at.gb_count(at.k // 2))
                V_.scalar_tensor_tensor(out=hg[:, at.k % H_RING, :], in0=ring(at)[:], scalar=neg_b1[:, at.k:at.k + 1],
                                        in1=gb[:, (at.k // 2) % GB_RING, :], op0=ALU.max, op1=ALU.mult).then_inc(d_done, 1)

            def back(at):
                xb = X[:, x_place(at), :, :].rearrange("p n d -> p (n d)")
                V_.tensor_tensor(xb, ring(at)[:], xb, ALU.add).then_inc(d_done, 1)

            def qk(at):
                slot = "qk".index(at.name)
                low(at, nat_l[:, slot, :], nat_h[:, slot, :])

            def max_(at):
                head, n = divmod(at.k, TILES)
                V_.tensor_reduce(neg_m[:, n, head:head + 1], ring(at)[:], AX.X, ALU.max, negate=True).then_inc(d_done, 1)

            def mrow(at):
                low(at, mrow_l[:], mrow_h[:])

            def onorm(at):
                dve.wait_ge(a_done, at.count("a_done", "sum"))
                chain(V_.tensor_tensor(o_n[:], o_n[:], rden[:], ALU.mult))
                chain(V_.scalar_tensor_tensor(out=rden[:], in0=o_n[:], scalar=-2.0, in1=rden[:], op0=ALU.add, op1=ALU.mult))
                dve.wait_ge(S["p_used"], at.count("p_used", "pv", (at.k + 1) * TILES - 1))
                V_.scalar_tensor_tensor(out=o_n[:], in0=o_bank[:], scalar=-1.0, in1=rden[:], op0=ALU.mult,
                                        op1=ALU.mult).then_inc(S["o_read"], 1)

            does = {"norm": norm, "scaled": scaled, "xT": xT, "logits": logits, "top1": top1, "top2": top2, "gT": gT_, "h": h, "back": back, "q": qk, "k": qk,
                    "max": max_, "mrow": mrow, "onorm": onorm}
            walk(dve, does, chain, {"xT": split_weights, "gb": split_more})

        @block.tensor
        def _(pe):
            def product3(dst, wh, wl, mh, ml, start=True, stop=True):
                pe_mm(dst, wh, mh, start=start, stop=False)
                pe_mm(dst, wl, mh, start=False, stop=False)
                return pe_mm(dst, wh, ml, start=False, stop=stop)

            def pe_mm(dst, w, m, start=True, stop=True):
                return nc.tensor.matmul(dst, w, m, start=start, stop=stop)

            def turn_weights():
                pe.wait_ge(weights_in, 16 * WEIGHT_DMAS)
                pe.wait_ge(consts_made, 1)
                nc.tensor.transpose(y_bank[:, 0:EXPERTS], gw_raw, ident[0:EXPERTS, 0:EXPERTS])
                nc.tensor.transpose(y_bank[:, EXPERTS:EXPERTS + UNITS], b1_raw, ident[0:UNITS, 0:UNITS])
                for g in range(GROUPS):
                    nc.tensor.transpose(o_bank[:, g * P:(g + 1) * P], wq_raw[:, g, :], ident[:])
                    nc.tensor.transpose(o_bank[:, HD + g * D:HD + (g + 1) * D], wo_raw[:, g * P:(g + 1) * P], ident[:])
                    nc.tensor.transpose(act_ring[1][0:RANK, g * P:(g + 1) * P], wk_raw[:, g, :], ident[:])
                    last = nc.tensor.transpose(act_ring[1][0:RANK, HD + g * P:HD + (g + 1) * P], wv_raw[:, g, :],
                                               ident[:])
                last.then_inc(setup_pe, 1)

            def multiply_weights():
                pe_mm(act_ring[0][:], down_raw, up_T)
                for u in range(UNITS):
                    last = pe_mm(act_ring[1][0:EXPERTS, 0:D], b1_masked[:, u, :], w2_sb[:, u, :],
                                 start=(u == 0), stop=(u == UNITS - 1))
                last.then_inc(setup_pe, 1)

            def ring_d(at):
                wait(pe, d_done, at.count("d_done", back=D_RING + ADDS["d_full"][at.name] - 1))
                return dve_ring[at.bank("d_full", D_RING)]

            def ring_a(at):
                wait(pe, a_done, at.count("a_done", back=A_RING + ADDS["a_full"][at.name] - 1))
                return act_ring[at.bank("a_full", A_RING)]

            def tokens(n):
                return slice(n * P, (n + 1) * P)

            def xT(at):
                bank = ring_d(at)
                pe.wait_ge(S["xn_done"], at.count("xn_done", "scaled", 0))
                for n in range(TILES):
                    last = nc.tensor.transpose(bank[:, tokens(n)], xn[at.stage][:, n, :], ident[:])
                last.then_inc(d_full, 1)

            def logits(at):
                bank = ring_d(at)
                pe.wait_ge(d_done, at.count("d_done", "xT", 0))
                for n in range(TILES):
                    last = product3(bank[:, n * EXPERTS:(n + 1) * EXPERTS], xT_h[at.stage][:, tokens(n)], xT_l[at.stage][:, tokens(n)],
                                    gw_h[:], gw_l[:])
                last.then_inc(d_full, 2)

            def gT_(at):
                bank = ring_d(at)
                pe.wait_ge(S["g_done"], at.count("g_done", "top2", 0))
                for n in range(TILES):
                    last = nc.tensor.transpose(bank[0:EXPERTS, tokens(n)], G[:, n, :], ident[:])
                last.then_inc(d_full, 1)

            def h(at):
                product3(ring_d(at)[:], w1h[:, at.k * P:(at.k + 1) * P], w1l[:, at.k * P:(at.k + 1) * P],
                         xT_h[at.stage][:], xT_l[at.stage][:]).then_inc(d_full, 1)

            def y(at):
                pe.wait_ge(d_done, at.count("d_done", "h"))
                if at.k == 0:
                    wait(pe, S["yT_done"], at.count("yT_done", "fix", 0, back=1))
                pe_mm(y_bank[:], w2_sb[:, at.k, :], hg[:, at.k % H_RING, :], start=at.k == 0,
                      stop=False).then_inc(S["y_used"], 1)

            def fix(at):
                pe_mm(y_bank[:], corr[:], gT[at.stage][:], start=False, stop=True).then_inc(S["y_full"], 1)

            def back(at):
                bank = ring_d(at)
                if at.stage == "B":
                    pe.wait_ge(a_done, at.count("a_done", "wo", 0))
                else:
                    pe.wait_ge(S["yT_done"], at.count("yT_done", "fix", 0))
                for n in range(TILES):
                    last = nc.tensor.transpose(bank[:, tokens(n)], (yT_B if at.stage == "B" else yT)[:, tokens(n)], ident[:])
                last.then_inc(d_full, 1)

            def qk(at):
                bank, kind, g = ring_d(at), "qk".index(at.name), at.k
                if at.k == 0:
                    pe.wait_ge(d_done, at.count("d_done", "xT", 0))
                product3(bank[:], wqkv_h[:, kind, g * P:(g + 1) * P], wqkv_l[:, kind, g * P:(g + 1) * P],
                         xT_h[at.stage][:], xT_l[at.stage][:]).then_inc(d_full, 1)

            def v(at):
                bank = ring_a(at)
                for i in range(2):
                    n = 2 * at.k + i
                    last = product3(bank[:, i * HD:(i + 1) * HD], xT_h[at.stage][:, tokens(n)], xT_l[at.stage][:, tokens(n)],
                                    wqkv_h[:, 2, :], wqkv_l[:, 2, :])
                last.then_inc(a_full, 1)

            def max_(at):
                head, n = divmod(at.k, TILES)
                bank = ring_d(at)
                if at.k % (GROUP * TILES) == 0:
                    pe.wait_ge(S["q_stacked"], at.count("q_stacked", "q", head // GROUP))
                    pe.wait_ge(S["k_stacked"], at.count("k_stacked", "k", head // GROUP))
                pe_mm(bank[:], qs[0:STACK, head, tokens(n)], ks[0:STACK, head, :]).then_inc(d_full, 1)

            def mrow(at):
                bank = ring_d(at)
                pe.wait_ge(d_done, at.count("d_done", "max", (at.k + 1) * GROUP * TILES - 1))
                for n in range(TILES):
                    last = nc.tensor.transpose(bank[0:GROUP, tokens(n)], neg_m[:, n, at.k * GROUP:(at.k + 1) * GROUP],
                                               ident[:])
                last.then_inc(d_full, 2)

            def s_(at):
                m, j = divmod(at.k, GROUP)
                g, kt = divmod(m, TILES)
                bank = ring_a(at)
                if kt == 0 and j == 0:
                    pe.wait_ge(S["m_stacked"], at.count("m_stacked", "mrow", g))
                head = g * GROUP + j
                pe_mm(bank[:], ks[:, head, tokens(kt)], qs[:, head, :]).then_inc(a_full, 1)

            def pv(at):
                g, kt = divmod(at.k, TILES)
                pe.wait_ge(a_done, at.count("a_done", "s", at.k * GROUP + GROUP - 1))
                if kt == 0:
                    wait(pe, S["o_read"], at.count("o_read", "onorm", g, back=1))
                for j in range(GROUP):
                    head = g * GROUP + j
                    last = nc.tensor.matmul(o_bank[j * DH:(j + 1) * DH, :], V[:, kt, head * DH:(head + 1) * DH],
                                            probs[:, at.k % P_RING, j, :], start=kt == 0, stop=kt == TILES - 1)
                last.then_inc(S["p_used"], 1)

            def sum_(at):
                bank = ring_a(at)
                pe.wait_ge(S["p_added"], at.count("p_added", "add", (at.k + 1) * TILES * GROUP - 1))
                for j in range(GROUP):
                    last = nc.tensor.matmul(bank[j * DH:(j + 1) * DH, :], ones[:], probs[:, TILES - 1, j, :], start=True, stop=True)
                last.then_inc(a_full, 1)

            def wo_(at):
                bank = ring_a(at)
                pe.wait_ge(S["o_done"], at.count("o_done", "oh", GROUPS - 1))
                for g in range(GROUPS):
                    last = product3(bank[:], wo_h[:, g, :], wo_l[:, g, :], o_h[:, g, :], o_l[:, g, :],
                                    start=g == 0, stop=g == GROUPS - 1)
                last.then_inc(a_full, 2)

            def gate_weights_split():
                pe.wait_ge(setup_dve, 1)

            def all_weights_split():
                pe.wait_ge(setup_dve, 2)

            setup = {"xT": turn_weights, "logits": gate_weights_split, "top1": multiply_weights,
                     "gb": all_weights_split}
            walk(pe, {"xT": xT, "logits": logits, "gT": gT_, "h": h, "y": y, "fix": fix, "back": back,
                      "q": qk, "k": qk, "v": v, "max": max_, "mrow": mrow, "s": s_, "pv": pv, "sum": sum_, "wo": wo_}, setup=setup)


_INS = ['L0_attn_x', 'L0_attn_Wq', 'L0_attn_Wkv_down', 'L0_attn_Wk_up', 'L0_attn_Wv_up', 'L0_attn_Wo',
        'L0_ffn_gate_w', 'L0_ffn_gate_b', 'L0_ffn_w1', 'L0_ffn_b1', 'L0_ffn_w2', 'L0_ffn_b2']


def kernel(**inputs):
    import numpy as _np
    import concourse.bacc as _bacc
    from concourse import mybir as _mybir
    from concourse.bass_utils import run_bass_kernel_spmd as _run

    nc = _bacc.Bacc("TRN2", target_bir_lowering=False, num_devices=1)
    arrays, args = {}, []
    for name in _INS:
        a = _np.ascontiguousarray(inputs[name])
        arrays[f"in_{name}_dram"] = a
        args.append(nc.dram_tensor(f"in_{name}_dram", a.shape, _mybir.dt.from_np(a.dtype), kind="ExternalInput").ap())
    shape = inputs['L0_attn_x'].shape
    args.append(nc.dram_tensor("out_0_dram", shape, _mybir.dt.float32, kind="ExternalOutput").ap())
    macaron_kernel(nc, *args)
    r = _run(nc, [arrays], core_ids=[0])
    return r.results[0]["out_0_dram"]
```
